# Optimizing a Trainium2 kernel written in Bass

```python
import numpy as np
import jax
import jax.numpy as jnp

def _softmax(x, axis=-1):
    return jax.nn.softmax(x, axis=axis)

def _gelu(x):
    return jax.nn.gelu(x, approximate=True)

def _silu(x):
    return jax.nn.silu(x)

def _sigmoid(x):
    return jax.nn.sigmoid(x)

def _layernorm(x, axis=-1, eps=1e-05):
    m = jnp.mean(x, axis=axis, keepdims=True)
    v = jnp.var(x, axis=axis, keepdims=True)
    return (x - m) / jnp.sqrt(v + eps)

def _scatter_add(tgt, idx, src, axis=0):
    return tgt.at[idx].add(src)

def _segment_sum(src, seg, n):
    return jax.ops.segment_sum(src, seg, n)
kernel_name = 'mk_decoder_postln_d1_seqx_r4_bf3e67'

def setup_inputs(seed: int=0):
    np.random.seed(seed)
    _w = jnp.asarray

    def _rec_inputs():
        import jax
        import jax.numpy as jnp
        _rk = jax.random.key(seed)
        x = 7.22e-05 + 1 * jax.random.normal(jax.random.fold_in(_rk, 1), (32, 256, 256), jnp.float32)
        _lenS = 256 - jax.random.randint(jax.random.fold_in(_rk, 7), (32,), 0, max(1, 256 // 4) + 1, jnp.int32)
        _lenS2 = 77 - jax.random.randint(jax.random.fold_in(_rk, 8), (32,), 0, max(1, 77 // 4) + 1, jnp.int32)
        fside_BxSxS_0 = 4.13588e-05 + 0.999923 * jax.random.normal(jax.random.fold_in(_rk, 11), (32, 256, 256), jnp.float32)
        _ctx_1024P = jax.random.normal(jax.random.fold_in(_rk, 13), (32, 16, 256), jnp.float32)
        _ctx_1024c = jax.random.dirichlet(jax.random.fold_in(_rk, 513), 0.3 * jnp.ones((16,), jnp.float32), (32, 77))
        _ctx_1024t = jnp.einsum('bsk,bkd->bsd', _ctx_1024c, _ctx_1024P)
        _ctx_1024t = _ctx_1024t * jax.lax.rsqrt(jnp.mean(jnp.square(_ctx_1024t)) + 1e-12) * 0.953939
        ctx_1024 = 0.00513834 + 0.998274 * (_ctx_1024t + 0.3 * jax.random.normal(jax.random.fold_in(_rk, 613), (32, 77, 256), jnp.float32))
        _validS = jnp.arange(256)[None, :] < _lenS[:, None]
        _validS2 = jnp.arange(77)[None, :] < _lenS2[:, None]
        _causal = jnp.tril(jnp.ones((256, 256), dtype=bool))
        mask_Bx16xSxS_bk1 = jnp.broadcast_to(_validS[:, None, None, :], (32, 16, 256, 256))
        return (x, fside_BxSxS_0, ctx_1024, mask_Bx16xSxS_bk1)
    x, fside_BxSxS_0, ctx_1024, mask_Bx16xSxS_bk1 = _rec_inputs()

    def _L0_attn_setup():
        import jax, jax.numpy as jnp
        import numpy as np
        B, N, C = (4, 1024, 256)
        H = 16
        D = C // H
        EPS = 1e-06

        def _feature_map(x):
            return jax.nn.elu(x) + 1.0
        key = jax.random.key(seed)
        k1, k2, k3, k4 = jax.random.split(key, 4)
        x = jax.random.normal(k1, (B, N, C), dtype=jnp.float32)
        Wqkv = jax.random.normal(k2, (3 * C, C), dtype=jnp.float32) * 0.02
        Wproj = jax.random.normal(k3, (C, C), dtype=jnp.float32) * 0.02
        bproj = jax.random.normal(k4, (C,), dtype=jnp.float32) * 0.02
        return {'x': x, 'Wqkv': Wqkv, 'Wproj': Wproj, 'bproj': bproj}
    _L0_attn_all = _L0_attn_setup()
    _L0_attn_in = {k: v for k, v in _L0_attn_all.items() if k in ('Wqkv', 'Wproj', 'bproj')}
    del _L0_attn_all

    def _L0_xattn_setup():
        import jax, jax.numpy as jnp
        import numpy as np
        D_MODEL, D_K, D_V, H = (256, 64, 64, 16)
        B, NQ, NK, M = (8, 256, 256, 49)

        def _xavier(key, shape):
            fan_in, fan_out = (shape[1], shape[0])
            limit = float(np.sqrt(6.0 / (fan_in + fan_out)))
            return jax.random.uniform(key, shape, jnp.float32, -limit, limit)
        key = jax.random.key(seed)
        ks = jax.random.split(key, 12)
        inp = {'queries': jax.random.normal(ks[0], (B, NQ, D_MODEL), jnp.float32), 'keys': jax.random.normal(ks[1], (B, NK, D_MODEL), jnp.float32), 'values': jax.random.normal(ks[2], (B, NK, D_MODEL), jnp.float32), 'attention_mask': jax.random.randint(ks[3], (B, H, NQ, NK), 0, 2) > 0, 'key_grid': jax.random.normal(ks[4], (B, M, D_MODEL), jnp.float32), 'value_grid': jax.random.normal(ks[5], (B, M, D_MODEL), jnp.float32), 'Wq': _xavier(ks[6], (H * D_K, D_MODEL)), 'bq': jnp.zeros((H * D_K,), jnp.float32), 'Wk': _xavier(ks[7], (H * D_K, D_MODEL)), 'bk': jnp.zeros((H * D_K,), jnp.float32), 'Wgk': _xavier(ks[8], (H * D_K, D_MODEL)), 'bgk': jnp.zeros((H * D_K,), jnp.float32), 'Wv': _xavier(ks[9], (H * D_V, D_MODEL)), 'bv': jnp.zeros((H * D_V,), jnp.float32), 'Wgv': _xavier(ks[10], (H * D_V, D_MODEL)), 'bgv': jnp.zeros((H * D_V,), jnp.float32), 'Wo': _xavier(ks[11], (D_MODEL, H * D_V)), 'bo': jnp.zeros((D_MODEL,), jnp.float32)}
        return inp
    _L0_xattn_all = _L0_xattn_setup()
    _L0_xattn_in = {k: v for k, v in _L0_xattn_all.items() if k in ('Wq', 'bq', 'Wk', 'bk', 'Wgk', 'bgk', 'Wv', 'bv', 'Wgv', 'bgv', 'Wo', 'bo')}
    del _L0_xattn_all

    def _L0_ffn_setup():
        import jax, jax.numpy as jnp
        import numpy as np
        B, L, H, E, I = (4, 512, 256, 8, 1024)
        S = B * L
        CAP_FACTOR_EVAL = 2.0
        MIN_CAP = 4
        _cap = int(np.floor(CAP_FACTOR_EVAL * S / E))
        _cap += _cap % 2
        CAPACITY = max(_cap, MIN_CAP)

        def _layer_norm(x, g, b, eps=1e-05):
            mu = x.mean(-1, keepdims=True)
            var = ((x - mu) ** 2).mean(-1, keepdims=True)
            return (x - mu) * jax.lax.rsqrt(var + eps) * g + b
        key = jax.random.key(seed)
        ks = jax.random.split(key, 8)
        gate_std = float(np.sqrt(0.1 / H))
        return {'inputs': jax.random.normal(ks[0], (B, L, H), jnp.float32), 'gate_weight': jax.random.normal(ks[1], (E, H), jnp.float32) * gate_std, 'ln_gamma': jnp.ones((H,), jnp.float32), 'ln_beta': jnp.zeros((H,), jnp.float32), 'wi': jax.random.normal(ks[2], (E, H, I), jnp.float32) * float(1.0 / np.sqrt(H)), 'wo': jax.random.normal(ks[3], (E, I, H), jnp.float32) * float(1.0 / np.sqrt(I)), 'conf_w1': jax.random.normal(ks[4], (H // 2, H), jnp.float32) * float(np.sqrt(2.0 / (H + H // 2))), 'conf_b1': -jnp.ones((H // 2,), jnp.float32), 'conf_w2': jax.random.normal(ks[5], (1, H // 2), jnp.float32) * float(np.sqrt(2.0 / (1 + H // 2))), 'conf_b2': -jnp.ones((1,), jnp.float32), 'comp_w': jax.random.normal(ks[6], (1, H), jnp.float32) * float(1.0 / np.sqrt(H)), 'comp_b': jnp.zeros((1,), jnp.float32)}
    _L0_ffn_all = _L0_ffn_setup()
    _L0_ffn_in = {k: v for k, v in _L0_ffn_all.items() if k in ('gate_weight', 'ln_gamma', 'ln_beta', 'wi', 'wo', 'conf_w1', 'conf_b1', 'conf_w2', 'conf_b2', 'comp_w', 'comp_b')}
    del _L0_ffn_all
    return {'x': x, 'fside_BxSxS_0': fside_BxSxS_0, 'ctx_1024': ctx_1024, 'mask_Bx16xSxS_bk1': mask_Bx16xSxS_bk1, 'L0_attn_Wqkv': _L0_attn_in['Wqkv'], 'L0_attn_Wproj': _L0_attn_in['Wproj'], 'L0_attn_bproj': _L0_attn_in['bproj'], 'L0_xattn_Wq': _L0_xattn_in['Wq'], 'L0_xattn_bq': _L0_xattn_in['bq'], 'L0_xattn_Wk': _L0_xattn_in['Wk'], 'L0_xattn_bk': _L0_xattn_in['bk'], 'L0_xattn_Wgk': _L0_xattn_in['Wgk'], 'L0_xattn_bgk': _L0_xattn_in['bgk'], 'L0_xattn_Wv': _L0_xattn_in['Wv'], 'L0_xattn_bv': _L0_xattn_in['bv'], 'L0_xattn_Wgv': _L0_xattn_in['Wgv'], 'L0_xattn_bgv': _L0_xattn_in['bgv'], 'L0_xattn_Wo': _L0_xattn_in['Wo'], 'L0_xattn_bo': _L0_xattn_in['bo'], 'L0_ffn_gate_weight': _L0_ffn_in['gate_weight'], 'L0_ffn_ln_gamma': _L0_ffn_in['ln_gamma'], 'L0_ffn_ln_beta': _L0_ffn_in['ln_beta'], 'L0_ffn_wi': _L0_ffn_in['wi'], 'L0_ffn_wo': _L0_ffn_in['wo'], 'L0_ffn_conf_w1': _L0_ffn_in['conf_w1'], 'L0_ffn_conf_b1': _L0_ffn_in['conf_b1'], 'L0_ffn_conf_w2': _L0_ffn_in['conf_w2'], 'L0_ffn_conf_b2': _L0_ffn_in['conf_b2'], 'L0_ffn_comp_w': _L0_ffn_in['comp_w'], 'L0_ffn_comp_b': _L0_ffn_in['comp_b']}

def reference(x, fside_BxSxS_0, ctx_1024, mask_Bx16xSxS_bk1, L0_attn_Wqkv, L0_attn_Wproj, L0_attn_bproj, L0_xattn_Wq, L0_xattn_bq, L0_xattn_Wk, L0_xattn_bk, L0_xattn_Wgk, L0_xattn_bgk, L0_xattn_Wv, L0_xattn_bv, L0_xattn_Wgv, L0_xattn_bgv, L0_xattn_Wo, L0_xattn_bo, L0_ffn_gate_weight, L0_ffn_ln_gamma, L0_ffn_ln_beta, L0_ffn_wi, L0_ffn_wo, L0_ffn_conf_w1, L0_ffn_conf_b1, L0_ffn_conf_w2, L0_ffn_conf_b2, L0_ffn_comp_w, L0_ffn_comp_b):
    import jax
    import jax.numpy as jnp

    def _L0_attn_ref(x, Wqkv, Wproj, bproj):
        import jax, jax.numpy as jnp
        import numpy as np
        B, N, C = (4, 1024, 256)
        H = 16
        D = C // H
        EPS = 1e-06

        def _feature_map(x):
            return jax.nn.elu(x) + 1.0
        b, n, c = x.shape
        qkv = jnp.einsum('bnc,fc->bnf', x, Wqkv).reshape(b, n, 3, H, D)
        qkv = jnp.transpose(qkv, (2, 0, 3, 1, 4))
        q, k, v = (qkv[0], qkv[1], qkv[2])
        q = _feature_map(q)
        k = _feature_map(k)
        kv = jnp.einsum('bhnd,bhne->bhde', k, v)
        k_sum = k.sum(axis=2)
        z = 1.0 / (jnp.einsum('bhnd,bhd->bhn', q, k_sum)[..., None] + EPS)
        out = jnp.einsum('bhnd,bhde->bhne', q, kv) * z
        out = jnp.transpose(out, (0, 2, 1, 3)).reshape(b, n, c)
        out = jnp.einsum('bnc,oc->bno', out, Wproj) + bproj
        return out

    def _L0_xattn_ref(queries, keys, values, attention_mask, key_grid, value_grid, Wq, bq, Wk, bk, Wgk, bgk, Wv, bv, Wgv, bgv, Wo, bo):
        import jax, jax.numpy as jnp
        import numpy as np
        D_MODEL, D_K, D_V, H = (256, 64, 64, 16)
        B, NQ, NK, M = (8, 256, 256, 49)

        def _xavier(key, shape):
            fan_in, fan_out = (shape[1], shape[0])
            limit = float(np.sqrt(6.0 / (fan_in + fan_out)))
            return jax.random.uniform(key, shape, jnp.float32, -limit, limit)
        b_s, nq, _ = queries.shape
        nk = keys.shape[1]
        scale = 1.0 / np.sqrt(D_K)
        k = keys @ Wk.T + bk
        gk = key_grid @ Wgk.T + bgk
        k_new = jnp.concatenate([k, gk], axis=1)
        k_new = k_new.reshape(b_s, -1, H, D_K).transpose(0, 2, 3, 1)
        v = values @ Wv.T + bv
        gv = key_grid @ Wgv.T + bgv
        v_new = jnp.concatenate([v, gv], axis=1)
        v_new = v_new.reshape(b_s, -1, H, D_V).transpose(0, 2, 1, 3)
        q = (queries @ Wq.T + bq).reshape(b_s, nq, H, D_K).transpose(0, 2, 1, 3)
        att = jnp.einsum('bhqd,bhdk->bhqk', q, k_new) * scale
        att_k = jnp.where(attention_mask, -jnp.inf, att[..., :nk])
        att = jnp.concatenate([att_k, att[..., nk:]], axis=-1)
        att = jax.nn.softmax(att, axis=-1)
        out = jnp.einsum('bhqk,bhkd->bhqd', att, v_new)
        out = out.transpose(0, 2, 1, 3).reshape(b_s, nq, H * D_V)
        return out @ Wo.T + bo

    def _L0_ffn_ref(inputs, gate_weight, ln_gamma, ln_beta, wi, wo, conf_w1, conf_b1, conf_w2, conf_b2, comp_w, comp_b):
        import jax, jax.numpy as jnp
        import numpy as np
        B, L, H, E, I = (4, 512, 256, 8, 1024)
        S = B * L
        CAP_FACTOR_EVAL = 2.0
        MIN_CAP = 4
        _cap = int(np.floor(CAP_FACTOR_EVAL * S / E))
        _cap += _cap % 2
        CAPACITY = max(_cap, MIN_CAP)

        def _layer_norm(x, g, b, eps=1e-05):
            mu = x.mean(-1, keepdims=True)
            var = ((x - mu) ** 2).mean(-1, keepdims=True)
            return (x - mu) * jax.lax.rsqrt(var + eps) * g + b
        tokens = inputs.reshape(-1, H)
        residual = tokens
        tokens = _layer_norm(tokens, ln_gamma, ln_beta)
        complexity_score = jax.nn.sigmoid(tokens @ comp_w.T + comp_b).mean()
        hdn = jax.nn.relu(tokens @ conf_w1.T + conf_b1)
        confidence_score = jax.nn.sigmoid(hdn @ conf_w2.T + conf_b2).mean()
        logits = tokens.astype(jnp.float32) @ gate_weight.astype(jnp.float32).T
        probs = jax.nn.softmax(logits, axis=-1)
        top1 = jnp.argmax(logits, axis=-1)
        onehot = jax.nn.one_hot(top1, E, dtype=jnp.int32)
        rank_e = jnp.cumsum(onehot, axis=0) - onehot
        rank = jnp.sum(rank_e * onehot, axis=-1)
        keep = rank < CAPACITY
        weight = jnp.take_along_axis(probs, top1[:, None], axis=-1)[:, 0]
        weight = (weight * keep).astype(tokens.dtype)
        slot = jnp.where(keep, rank, 0)
        dispatch = jnp.zeros((E, CAPACITY, H), tokens.dtype)
        dispatch = dispatch.at[top1, slot].add(tokens * keep[:, None])
        h = jax.nn.gelu(jnp.einsum('ech,ehi->eci', dispatch, wi), approximate=False)
        expert_out = jnp.einsum('eci,eih->ech', h, wo)
        combined = weight[:, None] * expert_out[top1, slot]
        out = (residual + combined).reshape(inputs.shape)
        return out
    x = _layernorm(x + _L0_attn_ref(x, L0_attn_Wqkv, L0_attn_Wproj, L0_attn_bproj), axis=-1)
    x = _layernorm(x + _L0_xattn_ref(x, fside_BxSxS_0, fside_BxSxS_0, mask_Bx16xSxS_bk1, ctx_1024, ctx_1024, L0_xattn_Wq, L0_xattn_bq, L0_xattn_Wk, L0_xattn_bk, L0_xattn_Wgk, L0_xattn_bgk, L0_xattn_Wv, L0_xattn_bv, L0_xattn_Wgv, L0_xattn_bgv, L0_xattn_Wo, L0_xattn_bo), axis=-1)
    x = _layernorm(x + _L0_ffn_ref(x, L0_ffn_gate_weight, L0_ffn_ln_gamma, L0_ffn_ln_beta, L0_ffn_wi, L0_ffn_wo, L0_ffn_conf_w1, L0_ffn_conf_b1, L0_ffn_conf_w2, L0_ffn_conf_b2, L0_ffn_comp_w, L0_ffn_comp_b), axis=-1)
    return x

_drawn_inputs = setup_inputs


def setup_inputs(seed=0):
    import zlib

    import numpy as np

    out = dict(_drawn_inputs(seed))
    spreads = {'L0_xattn_bq': (0.0, 0.75),
     'L0_xattn_bk': (0.0, 0.8),
     'L0_xattn_bgk': (0.0, 0.8),
     'L0_xattn_bv': (0.0, 0.1),
     'L0_xattn_bgv': (0.0, 0.1),
     'L0_xattn_bo': (0.0, 0.1),
     'L0_ffn_ln_gamma': (1.0, 0.6),
     'L0_ffn_ln_beta': (0.0, 0.402),
     'L0_ffn_conf_b1': (-1.0, 0.2)}
    factors = {'L0_attn_Wqkv': 7.737, 'L0_attn_Wproj': 7.4, 'L0_attn_bproj': 2.997, 'L0_xattn_Wk': 3.146}
    for name, (base, spread) in spreads.items():
        noise = np.random.default_rng([zlib.crc32(name.encode()), seed]).standard_normal(out[name].shape)
        drawn = base * np.exp(spread * noise) if base else spread * noise
        out[name] = jnp.asarray(drawn.astype(out[name].dtype))
    for name, factor in factors.items():
        out[name] = (out[name] * factor).astype(out[name].dtype)
    return out
```

```python
from contextlib import ExitStack

import concourse.bass as bass
from concourse import mybir

ALU = mybir.AluOpType
ACT = mybir.ActivationFunctionType
AX = mybir.AxisListType
F32 = mybir.dt.float32
BF16 = mybir.dt.bfloat16
U8 = mybir.dt.uint8
I32 = mybir.dt.int32
U32 = mybir.dt.uint32

P = 128
B, S, C = 32, 256, 256
TT = S // P
KC = C // P
LH, LD = 16, 16
HP = P // LD
XH, DK = 16, 64
XF = XH * DK
PAIRS = XH // 2
G = 77
NK = S + G
KT_TILES = (P, P, G)
PW = 3 * P
STEPS = XH * TT
E, I = 8, 1024
CAP = 512
ST = CAP // P
IT = I // P
TILES = B * TT
EPS_LIN = 1e-6
EPS_LN = 1e-5
MASKED = -1e30
SCALE = DK ** -0.5
NL = LD * HP + HP

GEN = (["lin_q0", "lin_q1", "lin_kv0", "lin_kv1", "k0", "k1", "lin_sum", "k2", "lin_out0", "lin_out1",
        "k3", "k4", "k5", "lin_proj", "k6", "k7", "v0", "v1", "v2", "v3", "v4", "v5"]
       + [f"q{j}" for j in range(PAIRS)] + ["o_proj0", "o_proj1"])
assert len(GEN) % 2 == 0
GB = len(GEN) // 2
ROUTER_TRN = ["tok_t", "logits", "rank"]
TRN = ROUTER_TRN + ["lin_t", "x1_t"] + [f"o_t{j}" for j in range(PAIRS)]
CHAIN = 14 + PAIRS
ROUTER_CHAIN = 13


def wait(eng, sem, value):
    if not isinstance(value, int) or value > 0:
        eng.wait_ge(sem, value)


def stand(eng, sem):
    eng.sem_inc(sem, 1)


def gen_at(b, name):
    n = GEN.index(name)
    return n % 2, b * GB + n // 2 + 1


def trn_at(b, name):
    return b * len(TRN) + TRN.index(name) - len(ROUTER_TRN) + 1


def chain(eng, sem, b, per_batch):
    done = [0]

    def link(ins):
        done[0] += 1
        assert done[0] <= per_batch
        ins.then_inc(sem, 1)
        eng.wait_ge(sem, b * per_batch + done[0])
    return link, done


def decoder_kernel(nc, io):
    with ExitStack() as keep:
        def dram(name, shape):
            return nc.dram_tensor(name, shape, F32, kind="Internal").ap()

        x2_dram = dram("x2_dram", [B, P, TT, C])
        slots_dram = dram("slots_dram", [E * CAP, C])
        rows_dram = dram("rows_dram", [E * CAP, C])

        consts = keep.enter_context(nc.sbuf_tensor("consts", [P, 3 * P + NL + E], F32))
        weight = keep.enter_context(nc.sbuf_tensor("weight", [P, TILES], F32))
        gather_at = keep.enter_context(nc.sbuf_tensor("gather_at", [P, TILES], I32))
        half_pow = keep.enter_context(nc.sbuf_tensor("half_pow", [P, TT], F32))
        attention_and_router(nc, io, consts, weight, gather_at, half_pow, x2_dram, slots_dram)
        experts(nc, io, consts, slots_dram, rows_dram)
        combine(nc, io, weight, gather_at, half_pow, x2_dram, rows_dram)


def attention_and_router(nc, io, consts, weight, gather_at, half_pow, x2_dram, slots_dram):
    with ExitStack() as ctx:
        def sb(name, shape, dt=F32):
            return ctx.enter_context(nc.sbuf_tensor(name, shape, dt))

        def sem(name):
            return ctx.enter_context(nc.semaphore(name))

        def bank(name):
            return ctx.enter_context(nc.psum_tensor(name, [P, 512], F32))

        ident = consts[:, 0:P]
        before = consts[:, P:2 * P]
        ones = consts[:, 2 * P:3 * P]
        own_head = consts[:, 3 * P:3 * P + NL]
        expert_no = consts[:, 3 * P + NL:3 * P + NL + E]

        wqkv = sb("wqkv", [P, KC, 3 * C])
        wproj = sb("wproj", [P, KC, C])
        wq = sb("wq", [P, KC, XF])
        wk = sb("wk", [P, KC, XF])
        wgk = sb("wgk", [P, KC, XF])
        wv = sb("wv", [P, KC, XF])
        wgv = sb("wgv", [P, KC, XF])
        wo = sb("wo", [P, PAIRS, C])
        wgate = sb("wgate", [P, KC, E])
        col_bias = sb("col_bias", [P, 3, PAIRS])
        row_bias = sb("row_bias", [P, 4, C])
        v_bias = sb("v_bias", [P, 2, XF])
        x_t = sb("x_t", [P, KC, S])
        x_in = sb("x_in", [P, TT, C])
        f_t = sb("f_t", [P, KC, NK])
        mask_in = sb("mask_in", [P, STEPS, S], U8)
        mask_add = sb("mask_add", [P, STEPS, NK], BF16)
        x_bias = sb("x_bias", [P, TT, C])
        e_x = sb("e_x", [P, 4, C])
        lin_q = sb("lin_q", [P, KC, S])
        lin_k = sb("lin_k", [P, TT, C])
        lin_v = sb("lin_v", [P, TT, KC, NL])
        lin_kv = sb("lin_kv", [P, KC, NL])
        lin_den = sb("lin_den", [P, TT, KC, HP])
        lin_a = sb("lin_a", [P, TT, C])
        lin_at = sb("lin_at", [P, KC, S])
        z = sb("z", [P, TT, C])
        stats = sb("stats", [P, TT, 6])
        mv = sb("mv", [P, TT, 2])
        var_eps = sb("var_eps", [P, TT])
        rstd = sb("rstd", [P, TT])
        x1 = sb("x1", [P, TT, C])
        x1_bias = sb("x1_bias", [P, TT, C])
        x1_t = sb("x1_t", [P, KC, S])
        q_z = sb("q_z", [P, XH, S])
        k_t = sb("k_t", [P, PAIRS, NK])
        v_s = sb("v_s", [P, 3, XF])
        masked = sb("masked", [P, 2, NK])
        low = sb("low", [P, STEPS])
        prob = sb("prob", [P, 3, PW])
        total = sb("total", [P, STEPS])
        inv_total = sb("inv_total", [P, 4])
        prob_t = sb("prob_t", [P, 2, PW])
        o_s = sb("o_s", [P, 2, TT, P])
        o_t = sb("o_t", [P, 2, S])
        x2 = sb("x2", [P, TT, C])
        normed = sb("normed", [P, TT, C])
        tok = sb("tok", [P, TT, C])
        tok_t = sb("tok_t", [P, KC, S])
        r_stats = sb("r_stats", [P, TT, 6])
        r_mv = sb("r_mv", [P, TT, 2])
        r_var = sb("r_var", [P, TT])
        r_rstd = sb("r_rstd", [P, TT])
        logit = sb("logit", [P, TT, E])
        top = sb("top", [P, TT, 8])
        top_at = sb("top_at", [P, TT, 8], U32)
        top_f = sb("top_f", [P, TT])
        rel = sb("rel", [P, TT, E])
        e_rel = sb("e_rel", [P, TT, E])
        e_sum = sb("e_sum", [P, TT])
        p_top = sb("p_top", [P, TT])
        onehot = sb("onehot", [P, TT, E])
        seen = sb("seen", [P, TT, E])
        own_rank = sb("own_rank", [P, TT, E])
        rank = sb("rank", [P, TT])
        kept_rank = sb("kept_rank", [P, TT])
        beyond = sb("beyond", [P, TT])
        slot_f = sb("slot_f", [P, TT])
        scatter_at = sb("scatter_at", [P, TT], I32)

        gen = [bank("gen0"), bank("gen1")]
        score = [bank("score0"), bank("score1")]
        prt = [bank("prt0"), bank("prt1")]
        out_ps = bank("out_ps")
        trn = bank("trn")

        consts_in, weights_in = sem("consts_in"), sem("weights_in")
        x_t_in, x_in_in, f_t_in, mask_in_in = sem("x_t_in"), sem("x_in_in"), sem("f_t_in"), sem("mask_in_in")
        slots_zeroed, scattered, x2_stored = sem("slots_zeroed"), sem("scattered"), sem("x2_stored")
        pool_zeros, dve_zeros = sem("pool_zeros"), sem("dve_zeros")
        gen_full = [sem("gen_full0"), sem("gen_full1")]
        gen_free = [sem("gen_free0"), sem("gen_free1")]
        trn_full, trn_free = sem("trn_full"), sem("trn_free")
        score_full, prt_full, out_full = sem("score_full"), sem("prt_full"), sem("out_full")
        exp_ready, lin_v_ready = sem("exp_ready"), sem("lin_v_ready")
        lin_a_ready = sem("lin_a_ready")
        x_bias_ready, x1_bias_ready = sem("x_bias_ready"), sem("x1_bias_ready")
        var_ready, rstd_ready = sem("var_ready"), sem("rstd_ready")
        x1_ready, x2_ready = sem("x1_ready"), sem("x2_ready")
        mask_ready, masked_ready = sem("mask_ready"), sem("masked_ready")
        prob_ready, prob_t_ready, o_ready = sem("prob_ready"), sem("prob_t_ready"), sem("o_ready")
        normed_ready, tok_ready = sem("normed_ready"), sem("tok_ready")
        r_var_ready, r_rstd_ready = sem("r_var_ready"), sem("r_rstd_ready")
        rel_ready, e_rel_ready = sem("rel_ready"), sem("e_rel_ready")
        seen_ready, scatter_ready = sem("seen_ready"), sem("scatter_ready")
        dve_chain, dve_router_chain = sem("dve_chain"), sem("dve_router_chain")
        pool_chain = sem("pool_chain")
        dve_stood, pool_stood, sp_stood = sem("dve_stood"), sem("pool_stood"), sem("sp_stood")

        block = ctx.enter_context(nc.Block())

        @block.sync
        def _(sp):
            sp.dma_start(consts[:, :], io["consts"]).then_inc(consts_in, 16)
            for dst, src in ((wqkv, "wqkv"), (wk, "wk"), (wgk, "wgk"), (wproj, "wproj"),
                             (wv, "wv"), (wgv, "wgv"), (wq, "wq"), (wo, "wo"), (wgate, "wgate"),
                             (col_bias, "col_bias"), (row_bias, "row_bias"), (v_bias, "v_bias")):
                sp.dma_start(dst[:, :, :], io[src]).then_inc(weights_in, 16)
            sp.wait_ge(pool_zeros, 1)
            slot_rows = slots_dram.rearrange("(n p t) c -> n p (t c)", p=P, t=TT)
            for n in range(E * CAP // (P * TT)):
                sp.dma_start(slot_rows[n], normed[:, :, :].rearrange("p t c -> p (t c)")).then_inc(slots_zeroed, 16)

            def load(b):
                wait(sp, gen_free[gen_at(0, "lin_kv1")[0]], gen_at(b - 1, "lin_kv1")[1] if not is_zero(b) else 0)
                stand(sp, sp_stood)
                sp.dma_start(x_t[:, :, :], batch_of(io["x_t"], b)).then_inc(x_t_in, 16)
                wait(sp, x_bias_ready, b)
                stand(sp, sp_stood)
                sp.dma_start(x_in[:, :, :], batch_of(io["x"], b)).then_inc(x_in_in, 16)
                wait(sp, mask_ready, PAIRS * b)
                stand(sp, sp_stood)
                sp.dma_start(mask_in[:, :, :], batch_of(io["mask"], b)).then_inc(mask_in_in, 16)
                wait(sp, gen_free[gen_at(0, "v5")[0]], gen_at(b - 1, "v5")[1] if not is_zero(b) else 0)
                stand(sp, sp_stood)
                sp.dma_start(f_t[:, :, :], batch_of(io["f_t"], b)).then_inc(f_t_in, 16)

            def store(b):
                sp.wait_ge(x2_ready, b + 1)
                stand(sp, sp_stood)
                sp.dma_start(batch_of(x2_dram, b), x2[:, :, :]).then_inc(x2_stored, 16)

            load(0)
            with sp.Fori(1, B) as b:
                load(b)
                store(b - 1)
            store(B - 1)
            sp.wait_ge(slots_zeroed, 16 * (E * CAP // (P * TT)))
            sp.wait_ge(x2_stored, 16 * B)

        @block.tensor
        def _(pe):
            def fill(b, name):
                k, n = gen_at(b, name)
                wait(pe, gen_free[k], n - 1)
                return gen[k], gen_full[k]

            def project(b, name, parts):
                ps, full = fill(b, name)
                for (c0, c1), lhs, rhs in parts:
                    for k in range(KC):
                        mm = pe.matmul(ps[0:lhs.shape[-1], c0:c1], lhs[:, k], rhs[:, k],
                                       start=(k == 0), stop=(k == KC - 1))
                mm.then_inc(full, 1)

            def keys(b, j):
                f = slice(j * P, j * P + P)
                project(b, f"k{j}", [((0, S), wk[:, :, f], f_t[:, :, 0:S]),
                                     ((S, NK), wgk[:, :, f], f_t[:, :, S:NK])])

            def values(b, n):
                t, half = n // 2, n % 2
                f = slice(half * 512, half * 512 + 512)
                w = wv if t < 2 else wgv
                project(b, f"v{n}", [((0, 512), f_t[:, :, t * P:t * P + KT_TILES[t]], w[:, :, f])])

            def transposes(b, src, name):
                wait(pe, trn_free, trn_at(b, name) - 1)
                for k in range(KC):
                    for t in range(TT):
                        mm = pe.transpose(trn[:, (k * TT + t) * P:(k * TT + t + 1) * P],
                                          src[:, t, k * P:k * P + P], ident)
                mm.then_inc(trn_full, 1)

            def router_tokens(r):
                pe.wait_ge(tok_ready, r + 1)
                transposes(r + 1, tok, "tok_t")

            def router_logits(r):
                pe.wait_ge(trn_free, trn_at(r + 1, "tok_t"))
                for t in range(TT):
                    for k in range(KC):
                        mm = pe.matmul(trn[:, t * E:t * E + E], tok_t[:, k, t * P:t * P + P], wgate[:, k, :],
                                       start=(k == 0), stop=(k == KC - 1))
                mm.then_inc(trn_full, 1)

            def router_rank(r):
                pe.wait_ge(seen_ready, r + 1)
                pe.matmul(trn[:, 0:TT * E], before, onehot[:, :, :], start=True, stop=False)
                pe.matmul(trn[:, 0:TT * E], ones, seen[:, :, :], start=False, stop=True).then_inc(trn_full, 1)

            def attend(b):
                for s in range(STEPS + 12):
                    if s < STEPS:
                        h, t = s // TT, s % TT
                        wait(pe, masked_ready, STEPS * b + s - 1)
                        pe.matmul(score[s % 2][:, 0:NK], q_z[:, h, t * P:t * P + P], k_t[:, h // 2, :],
                                  start=True, stop=True).then_inc(score_full, 1)
                    n = s - 2
                    if 0 <= n < STEPS:
                        wait(pe, prob_t_ready, STEPS * b + n - 1)
                        pe.wait_ge(prob_ready, STEPS * b + n + 1)
                        for k in range(3):
                            mm = pe.transpose(prt[n % 2][:, k * P:k * P + P], prob[:, n % 3, k * P:k * P + P], ident)
                        mm.then_inc(prt_full, 1)
                    n = s - 4
                    if 0 <= n < STEPS:
                        h, c = n // TT, n % 4
                        if c == 0:
                            wait(pe, o_ready, PAIRS * b + n // 4)
                        pe.wait_ge(prob_t_ready, STEPS * b + n + 1)
                        for k in range(3):
                            rows = KT_TILES[k]
                            mm = pe.matmul(out_ps[:, c * DK:c * DK + DK], prob_t[0:rows, n % 2, k * P:k * P + P],
                                           v_s[0:rows, k, h * DK:h * DK + DK], start=(k == 0), stop=(k == 2))
                        mm.then_inc(out_full, 1)
                    j, r = divmod(s - 9, 4)
                    if 0 <= j < PAIRS and r == 0:
                        wait(pe, trn_free, trn_at(b, f"o_t{j}") - 1)
                        pe.wait_ge(o_ready, PAIRS * b + j + 1)
                        for t in range(TT):
                            mm = pe.transpose(trn[:, t * P:t * P + P], o_s[:, j % 2, t, :], ident)
                        mm.then_inc(trn_full, 1)
                    j, r = divmod(s - 11, 4)
                    if 0 <= j < PAIRS and r == 0:
                        pe.wait_ge(trn_free, trn_at(b, f"o_t{j}"))
                        for t in range(TT):
                            ps, full = fill(b, f"o_proj{t}") if j == 0 else (gen[gen_at(0, f"o_proj{t}")[0]], None)
                            mm = pe.matmul(ps[:, 0:C], o_t[:, j % 2, t * P:t * P + P], wo[:, j, :],
                                           start=(j == 0), stop=(j == PAIRS - 1))
                            if j == PAIRS - 1:
                                mm.then_inc(gen_full[gen_at(0, f"o_proj{t}")[0]], 1)

            def batch(b):
                router = not is_zero(b)
                pe.wait_ge(x_t_in, 16 * b + 16)
                for k in range(KC):
                    project(b, f"lin_q{k}", [((0, S), wqkv[:, :, k * P:k * P + P], x_t)])
                for t in range(TT):
                    project(b, f"lin_kv{t}", [((0, 512), x_t[:, :, t * P:t * P + P], wqkv[:, :, C:3 * C])])
                if router:
                    router_tokens(b - 1)
                pe.wait_ge(f_t_in, 16 * b + 16)
                keys(b, 0)
                keys(b, 1)
                if router:
                    router_logits(b - 1)
                ps, full = fill(b, "lin_sum")
                k, n = gen_at(b, "lin_kv0")
                pe.wait_ge(gen_free[k], n)
                k, n = gen_at(b, "lin_kv1")
                pe.wait_ge(gen_free[k], n)
                for k in range(KC):
                    for t in range(TT):
                        mm = pe.matmul(ps[:, k * NL:k * NL + NL], lin_k[:, t, k * P:k * P + P], lin_v[:, t, k, :],
                                       start=(t == 0), stop=(t == TT - 1))
                mm.then_inc(full, 1)
                keys(b, 2)
                k, n = gen_at(b, "lin_sum")
                pe.wait_ge(gen_free[k], n)
                for t in range(TT):
                    ps, full = fill(b, f"lin_out{t}")
                    for k in range(KC):
                        mm = pe.matmul(ps[:, k * NL:k * NL + NL], lin_q[:, k, t * P:t * P + P], lin_kv[:, k, :],
                                       start=True, stop=True)
                    mm.then_inc(full, 1)
                keys(b, 3)
                if router:
                    router_rank(b - 1)
                keys(b, 4)
                pe.wait_ge(lin_a_ready, TT * b + TT)
                transposes(b, lin_a, "lin_t")
                keys(b, 5)
                pe.wait_ge(trn_free, trn_at(b, "lin_t"))
                project(b, "lin_proj", [((t * C, t * C + C), lin_at[:, :, t * P:t * P + P], wproj) for t in range(TT)])
                keys(b, 6)
                keys(b, 7)
                for n in range(6):
                    values(b, n)
                pe.wait_ge(x1_ready, b + 1)
                transposes(b, x1, "x1_t")
                pe.wait_ge(trn_free, trn_at(b, "x1_t"))
                for j in range(PAIRS):
                    project(b, f"q{j}", [((0, S), wq[:, :, j * P:j * P + P], x1_t)])
                for name in ("k7", "v4", "v5", "q6", "q7"):
                    k, n = gen_at(b, name)
                    pe.wait_ge(gen_free[k], n)
                attend(b)

            pe.wait_ge(consts_in, 16)
            pe.wait_ge(weights_in, 12 * 16)
            pe.wait_ge(pool_zeros, 3)
            pe.wait_ge(dve_zeros, 2)
            batch(0)
            with pe.Fori(1, B) as b:
                batch(b)
            router_tokens(B - 1)
            router_logits(B - 1)
            router_rank(B - 1)

        @block.scalar
        def _(act):
            def own(name, b):
                k, n = gen_at(b, name)
                act.wait_ge(gen_full[k], n)
                return gen[k], gen_free[k]

            def keys(b, j):
                ps, free = own(f"k{j}", b)
                act.activation(k_t[:, j, 0:S], ps[:, 0:S], ACT.Identity, bias=col_bias[:, 1, j:j + 1])
                act.activation(k_t[:, j, S:NK], ps[:, S:NK], ACT.Identity, bias=col_bias[:, 2, j:j + 1]).then_inc(free, 1)

            def from_trn(b, name, dst, cols=512):
                act.wait_ge(trn_full, trn_at(b, name))
                act.activation(dst, trn[:, 0:cols], ACT.Copy).then_inc(trn_free, 1)

            def flat(t):
                return t[:, :, :].rearrange("p a b -> p (a b)")

            def router_exp(r):
                act.wait_ge(rel_ready, r + 1)
                act.activation(e_rel[:, :, :], rel[:, :, :], ACT.Exp).then_inc(e_rel_ready, 1)

            def batch(b):
                router = not is_zero(b)
                for k in range(KC):
                    ps, free = own(f"lin_q{k}", b)
                    act.activation(e_x[:, k, :], ps[:, 0:C], ACT.Exp).then_inc(exp_ready, 1)
                for t in range(TT):
                    ps, free = own(f"lin_kv{t}", b)
                    act.activation(lin_v[:, t, :, 0:P], ps[:, C:2 * C].rearrange("p (k c) -> p k c", k=KC), ACT.Copy)
                    act.activation(e_x[:, KC + t, :], ps[:, 0:C], ACT.Exp).then_inc(exp_ready, 1)
                if router:
                    from_trn(b, "tok_t", flat(tok_t))
                keys(b, 0)
                keys(b, 1)
                keys(b, 2)
                if router:
                    router_exp(b - 1)
                keys(b, 3)
                keys(b, 4)
                from_trn(b, "lin_t", flat(lin_at))
                keys(b, 5)
                keys(b, 6)
                keys(b, 7)
                from_trn(b, "x1_t", flat(x1_t))
                for s in range(STEPS + 12):
                    if s < STEPS:
                        wait(act, prt_full, STEPS * b + s - 2)
                        act.wait_ge(masked_ready, STEPS * b + s + 1)
                        act.activation(prob[:, s % 3, 0:NK], masked[:, s % 2, :], ACT.Exp, bias=low[:, s:s + 1],
                                       scale=-1.0, accum_out=total[:, s:s + 1]).then_inc(prob_ready, 1)
                    n = s - 2
                    if 0 <= n < STEPS:
                        wait(act, out_full, STEPS * b + n - 1)
                        act.wait_ge(prt_full, STEPS * b + n + 1)
                        act.activation(prob_t[:, n % 2, :], prt[n % 2][:, 0:PW], ACT.Copy).then_inc(prob_t_ready, 1)
                    j, r = divmod(s - 10, 4)
                    if 0 <= j < PAIRS and r == 0:
                        from_trn(b, f"o_t{j}", o_t[:, j % 2, :], S)

            act.wait_ge(weights_in, 12 * 16)
            act.wait_ge(pool_zeros, 3)
            batch(0)
            with act.Fori(1, B) as b:
                batch(b)
            from_trn(B, "tok_t", flat(tok_t))
            router_exp(B - 1)

        @block.vector
        def _(dve):
            def own(name, b):
                k, n = gen_at(b, name)
                dve.wait_ge(gen_full[k], n)
                return gen[k], gen_free[k]

            def feature(b, n, name, dst, link):
                ps, free = own(name, b)
                dve.wait_ge(exp_ready, 4 * b + n + 1)
                link(dve.tensor_scalar(e_x[:, n, :], e_x[:, n, :], 1.0, None, ALU.min))
                dve.scalar_tensor_tensor(out=dst, in0=ps[:, 0:C], scalar=0.0, in1=e_x[:, n, :],
                                         op0=ALU.max, op1=ALU.add).then_inc(free, 1)

            def moments(src, st, m, var, link, ready):
                for t in range(TT):
                    last = dve.bn_stats(st[:, t, :], src[:, t, :])
                link(last)
                stand(dve, dve_stood)
                for t in range(TT):
                    last = dve.bn_aggr(m[:, t, :], st[:, t, :])
                link(last)
                dve.tensor_scalar(var[:, :], m[:, :, 1], EPS_LN, None, ALU.add).then_inc(ready, 1)

            def normalise(dst, src, m, rs, ready):
                for t in range(TT):
                    last = dve.tensor_scalar(dst[:, t, :], src[:, t, :], m[:, t, 0:1], rs[:, t:t + 1],
                                             ALU.subtract, ALU.mult)
                last.then_inc(ready, 1)

            def router_choice(r, link):
                dve.wait_ge(trn_full, trn_at(r + 1, "logits"))
                ins = dve.tensor_copy(logit[:, :, :], trn[:, 0:TT * E].rearrange("p (t e) -> p t e", e=E))
                ins.then_inc(trn_free, 1)
                dve.wait_ge(trn_free, trn_at(r + 1, "logits"))
                stand(dve, dve_stood)
                for t in range(TT):
                    last = dve.max(top[:, t, :], logit[:, t, :])
                link(last)
                dve.tensor_tensor(rel[:, :, :], logit[:, :, :], top[:, :, 0:1].to_broadcast([P, TT, E]),
                                  ALU.subtract).then_inc(rel_ready, 1)
                for t in range(TT):
                    last = dve.max_index(top_at[:, t, :], top[:, t, :], logit[:, t, :])
                link(last)
                link(dve.tensor_copy(top_f[:, :], top_at[:, :, 0]))
                link(dve.tensor_tensor(onehot[:, :, :], expert_no.unsqueeze(1).to_broadcast([P, TT, E]),
                                       top_f[:, :].unsqueeze(2).to_broadcast([P, TT, E]), ALU.is_equal))
                dve.tensor_tensor(seen[:, 1, :], seen[:, 0, :], onehot[:, 0, :], ALU.add).then_inc(seen_ready, 1)
                dve.wait_ge(e_rel_ready, r + 1)
                link(dve.tensor_reduce(e_sum[:, :], e_rel[:, :, :], AX.X, ALU.add))
                link(dve.reciprocal(p_top[:, :], e_sum[:, :]))

            def router_slots(r, link):
                dve.wait_ge(trn_full, trn_at(r + 1, "rank"))
                ins = dve.tensor_tensor(own_rank[:, :, :], trn[:, 0:TT * E].rearrange("p (t e) -> p t e", e=E),
                                        onehot[:, :, :], ALU.mult)
                ins.then_inc(trn_free, 1)
                dve.wait_ge(trn_free, trn_at(r + 1, "rank"))
                link(dve.tensor_reduce(rank[:, :], own_rank[:, :, :], AX.X, ALU.add))
                link(dve.tensor_tensor(seen[:, 0, :], seen[:, 1, :], onehot[:, 1, :], ALU.add))
                link(dve.scalar_tensor_tensor(out=kept_rank[:, :], in0=rank[:, :], scalar=float(CAP), in1=rank[:, :],
                                              op0=ALU.is_lt, op1=ALU.mult))
                link(dve.tensor_scalar(beyond[:, :], rank[:, :], float(CAP), float(2 * E * CAP), ALU.is_ge, ALU.mult))
                link(dve.scalar_tensor_tensor(out=slot_f[:, :], in0=top_f[:, :], scalar=float(CAP), in1=kept_rank[:, :],
                                              op0=ALU.mult, op1=ALU.add))
                if not is_zero(r):
                    dve.wait_ge(scattered, 32 * r)
                dve.tensor_tensor(scatter_at[:, :], slot_f[:, :], beyond[:, :], ALU.add).then_inc(scatter_ready, 1)
                link(dve.tensor_copy(gather_at[:, bass.ds(r * TT, TT)], slot_f[:, :]))
                link(dve.scalar_tensor_tensor(out=weight[:, bass.ds(r * TT, TT)], in0=rank[:, :], scalar=float(CAP),
                                              in1=p_top[:, :], op0=ALU.is_lt, op1=ALU.mult))

            def values(b, n):
                t, half = n // 2, n % 2
                rows = KT_TILES[t]
                cols = slice(half * 512, half * 512 + 512)
                ps, free = own(f"v{n}", b)
                dve.tensor_tensor(v_s[0:rows, t, cols], ps[0:rows, :], v_bias[0:rows, t // 2, cols],
                                  ALU.add).then_inc(free, 1)

            def batch(b):
                router = not is_zero(b)
                link, done = chain(dve, dve_chain, b, CHAIN)
                if router:
                    rlink, rdone = chain(dve, dve_router_chain, b - 1, ROUTER_CHAIN)
                for k in range(KC):
                    feature(b, k, f"lin_q{k}", lin_q[:, k, :], link)
                if router:
                    dve.wait_ge(r_rstd_ready, b)
                    normalise(normed, x2, r_mv, r_rstd, normed_ready)
                for t in range(TT):
                    feature(b, KC + t, f"lin_kv{t}", lin_k[:, t, :], link)
                if router:
                    router_choice(b - 1, rlink)
                ps, free = own("lin_sum", b)
                for k in range(KC):
                    last = dve.tensor_tensor(lin_kv[:, k, :], ps[:, k * NL:k * NL + NL], own_head, ALU.mult)
                last.then_inc(free, 1)
                for t in range(TT):
                    ps, free = own(f"lin_out{t}", b)
                    sums = ps[:, 0:KC * NL].rearrange("p (k c) -> p k c", k=KC)
                    link(dve.tensor_scalar(lin_den[:, t, :, :], sums[:, :, P:NL], EPS_LIN, None, ALU.add))
                    link(dve.reciprocal(lin_den[:, t, :, :], lin_den[:, t, :, :]))
                    for k in range(KC):
                        last = dve.tensor_tensor(
                            lin_a[:, t, k * P:k * P + P].rearrange("p (h d) -> p h d", d=LD),
                            ps[:, k * NL:k * NL + P].rearrange("p (h d) -> p h d", d=LD),
                            lin_den[:, t, k, :].unsqueeze(2).to_broadcast([P, HP, LD]), ALU.mult)
                    last.then_inc(free, 1)
                    k, n = gen_at(b, f"lin_out{t}")
                    dve.wait_ge(gen_free[k], n)
                    dve.sem_inc(lin_a_ready, 1)
                if router:
                    router_slots(b - 1, rlink)
                    assert rdone[0] == ROUTER_CHAIN, rdone
                ps, free = own("lin_proj", b)
                dve.wait_ge(x_bias_ready, b + 1)
                dve.tensor_tensor(z[:, :, :], ps[:, :].rearrange("p (t c) -> p t c", t=TT), x_bias[:, :, :],
                                  ALU.add).then_inc(free, 1)
                k, n = gen_at(b, "lin_proj")
                dve.wait_ge(gen_free[k], n)
                moments(z, stats, mv, var_eps, link, var_ready)
                values(b, 0)
                values(b, 1)
                dve.wait_ge(rstd_ready, 2 * b + 1)
                normalise(x1, z, mv, rstd, x1_ready)
                for n in range(2, 6):
                    values(b, n)
                for j in range(PAIRS):
                    ps, free = own(f"q{j}", b)
                    for i in range(2):
                        rows = slice(i * DK, i * DK + DK)
                        last = dve.tensor_scalar(q_z[rows, 2 * j + i, :], ps[rows, 0:S], col_bias[rows, 0, j:j + 1],
                                                 None, ALU.add)
                    last.then_inc(free, 1)
                for s in range(STEPS + 5):
                    j, r = divmod(s - 8, 4)
                    if 0 <= j < PAIRS and r == 0:
                        dve.wait_ge(out_full, STEPS * b + 4 * j + 4)
                        link(dve.reciprocal(inv_total[:, :], total[:, 4 * j:4 * j + 4]))
                        if j >= 2:
                            dve.wait_ge(trn_full, trn_at(b, f"o_t{j - 2}"))
                        for i in range(2):
                            last = dve.tensor_tensor(
                                o_s[:, j % 2, :, i * DK:i * DK + DK],
                                out_ps[:, i * P:i * P + P].rearrange("p (t d) -> p t d", t=TT),
                                inv_total[:, 2 * i:2 * i + 2].unsqueeze(2).to_broadcast([P, TT, DK]), ALU.mult)
                        last.then_inc(o_ready, 1)
                    if s < STEPS:
                        wait(dve, prob_ready, STEPS * b + s - 1)
                        if s % 4 == 0:
                            dve.wait_ge(mask_ready, PAIRS * b + s // 4 + 1)
                        dve.wait_ge(score_full, STEPS * b + s + 1)
                        stand(dve, dve_stood)
                        dve.tensor_tensor_reduce(masked[:, s % 2, :], score[s % 2][:, 0:NK], mask_add[:, s, :],
                                                 -SCALE, 3e38, ALU.add, ALU.min, low[:, s:s + 1]).then_inc(masked_ready, 1)
                dve.wait_ge(x1_bias_ready, b + 1)
                for t in range(TT):
                    ps, free = own(f"o_proj{t}", b)
                    dve.tensor_tensor(z[:, t, :], ps[:, 0:C], x1_bias[:, t, :], ALU.add).then_inc(free, 1)
                    k, n = gen_at(b, f"o_proj{t}")
                    dve.wait_ge(gen_free[k], n)
                moments(z, stats, mv, var_eps, link, var_ready)
                if not is_zero(b):
                    dve.wait_ge(x2_stored, 16 * b)
                dve.wait_ge(rstd_ready, 2 * b + 2)
                normalise(x2, z, mv, rstd, x2_ready)
                dve.wait_ge(x2_ready, b + 1)
                moments(x2, r_stats, r_mv, r_var, link, r_var_ready)
                assert done[0] == CHAIN, done

            dve.memset(q_z[:, :, :], 0.0).then_inc(dve_zeros, 1)
            dve.memset(seen[:, :, :], 0.0).then_inc(dve_zeros, 1)
            dve.wait_ge(dve_zeros, 2)
            dve.wait_ge(consts_in, 16)
            dve.wait_ge(weights_in, 12 * 16)
            batch(0)
            with dve.Fori(1, B) as b:
                batch(b)
            dve.wait_ge(r_rstd_ready, B)
            normalise(normed, x2, r_mv, r_rstd, normed_ready)
            rlink, _ = chain(dve, dve_router_chain, B - 1, ROUTER_CHAIN)
            router_choice(B - 1, rlink)
            router_slots(B - 1, rlink)

        @block.gpsimd
        def _(pool):
            def power(dst, src, ready):
                pool.tensor_tensor(dst[:, :], src[:, :], half_pow[:, :], ALU.pow).then_inc(ready, 1)

            def mask(b, j):
                n = slice(4 * j, 4 * j + 4)
                wait(pool, masked_ready, STEPS * (b - 1) + 4 * j + 4 if not is_zero(b) else 0)
                stand(pool, pool_stood)
                pool.tensor_scalar(mask_add[:, n, 0:S], mask_in[:, n, :], MASKED, 1.0, ALU.mult,
                                   ALU.mult).then_inc(mask_ready, 1)

            def router_root(r):
                pool.wait_ge(r_var_ready, r + 1)
                power(r_rstd, r_var, r_rstd_ready)

            def router_affine(r):
                pool.wait_ge(normed_ready, r + 1)
                wait(pool, scattered, 32 * r)
                for t in range(TT):
                    last = pool.tensor_tensor(tok[:, t, :], normed[:, t, :], row_bias[:, 2, :], ALU.mult)
                last.then_inc(pool_chain, 1)
                pool.wait_ge(pool_chain, r + 1)
                for t in range(TT):
                    last = pool.tensor_tensor(tok[:, t, :], tok[:, t, :], row_bias[:, 3, :], ALU.add)
                last.then_inc(tok_ready, 1)

            def router_scatter(r):
                pool.wait_ge(scatter_ready, r + 1)
                pool.wait_ge(tok_ready, r + 1)
                stand(pool, pool_stood)
                for t in range(TT):
                    pool.indirect_dma_start(
                        out=slots_dram, out_offset=bass.IndirectOffsetOnAxis(ap=scatter_at[:, t:t + 1], axis=0),
                        in_=tok[:, t, :], in_offset=None, bounds_check=last_slot, oob_is_err=False
                    ).then_inc(scattered, 16)

            def batch(b):
                router = not is_zero(b)
                if router:
                    router_root(b - 1)
                pool.wait_ge(x_in_in, 16 * b + 16)
                for t in range(TT):
                    last = pool.tensor_tensor(x_bias[:, t, :], x_in[:, t, :], row_bias[:, 0, :], ALU.add)
                last.then_inc(x_bias_ready, 1)
                if router:
                    router_affine(b - 1)
                pool.wait_ge(mask_in_in, 16 * b + 16)
                for j in range(3):
                    mask(b, j)
                pool.wait_ge(var_ready, 2 * b + 1)
                power(rstd, var_eps, rstd_ready)
                if router:
                    router_scatter(b - 1)
                pool.wait_ge(x1_ready, b + 1)
                for t in range(TT):
                    last = pool.tensor_tensor(x1_bias[:, t, :], x1[:, t, :], row_bias[:, 1, :], ALU.add)
                last.then_inc(x1_bias_ready, 1)
                for j in range(3, PAIRS):
                    mask(b, j)
                pool.wait_ge(var_ready, 2 * b + 2)
                power(rstd, var_eps, rstd_ready)

            last_slot = pool.to_reg(E * CAP - 1)
            pool.memset(normed[:, :, :], 0.0).then_inc(pool_zeros, 1)
            pool.memset(half_pow[:, :], -0.5)
            pool.memset(mask_add[:, :, S:NK], 0.0)
            pool.memset(prob[:, :, NK:PW], 0.0).then_inc(pool_zeros, 1)
            pool.memset(lin_v[:, :, :, P:NL], 1.0).then_inc(pool_zeros, 1)
            pool.wait_ge(pool_zeros, 3)
            pool.wait_ge(weights_in, 12 * 16)
            pool.wait_ge(slots_zeroed, 16 * (E * CAP // (P * TT)))
            batch(0)
            with pool.Fori(1, B) as b:
                batch(b)
            router_root(B - 1)
            router_affine(B - 1)
            router_scatter(B - 1)
            pool.wait_ge(scattered, 32 * B)


def is_zero(b):
    return isinstance(b, int) and b == 0


def batch_of(ap, b):
    return ap[bass.ds(b, 1)].rearrange("b p r c -> p (b r) c")


def experts(nc, io, consts, slots_dram, rows_dram):
    with ExitStack() as ctx:
        def sb(name, shape, dt=F32):
            return ctx.enter_context(nc.sbuf_tensor(name, shape, dt))

        def sem(name):
            return ctx.enter_context(nc.semaphore(name))

        ident = consts[:, 0:P]
        wi = [sb(f"wi{i}", [P, KC, I]) for i in range(2)]
        wo = [sb(f"wo_e{i}", [P, IT, C]) for i in range(2)]
        slots = [sb(f"slots{i}", [P, ST, C]) for i in range(2)]
        slots_t = sb("slots_t", [P, KC, CAP])
        hidden = sb("hidden", [P, IT, CAP])
        rows = sb("rows", [P, ST, C])
        ps_t = [ctx.enter_context(nc.psum_tensor(f"ps_t{i}", [P, 512], F32)) for i in range(2)]
        ps_h = [ctx.enter_context(nc.psum_tensor(f"ps_h{i}", [P, 512], F32)) for i in range(2)]
        ps_o = [ctx.enter_context(nc.psum_tensor(f"ps_o{i}", [P, 512], F32)) for i in range(2)]
        loaded = [sem("loaded0"), sem("loaded1")]
        t_full, t_ready = sem("t_full"), sem("t_ready")
        h_full, h_ready = sem("h_full"), sem("h_ready")
        o_full, o_ready = sem("o_full_e"), sem("o_ready_e")
        rows_stored, e_stood = sem("rows_stored"), sem("e_stood")
        PER = 3 * 16
        slot_tiles = slots_dram.rearrange("(e t p) c -> e p t c", t=ST, p=P)
        row_tiles = rows_dram.rearrange("(e t p) c -> e p t c", t=ST, p=P)

        block = ctx.enter_context(nc.Block())

        @block.sync
        def _(sp):
            def load(g, i):
                sp.dma_start(slots[i][:, :, :], batch_of(slot_tiles, 2 * g + i)).then_inc(loaded[i], 16)
                sp.dma_start(wi[i][:, :, :], batch_of(io["wi"], 2 * g + i)).then_inc(loaded[i], 16)
                sp.dma_start(wo[i][:, :, :], batch_of(io["wo_e"], 2 * g + i)).then_inc(loaded[i], 16)

            def store(g, i):
                e = 2 * g + i
                sp.wait_ge(o_ready, 2 * e + 2)
                stand(sp, e_stood)
                sp.dma_start(batch_of(row_tiles, e), rows[:, :, :]).then_inc(rows_stored, 16)

            load(0, 0)
            load(0, 1)
            with sp.Fori(1, E // 2) as g:
                for i in range(2):
                    store(g - 1, i)
                    load(g, i)
            store(E // 2 - 1, 0)
            store(E // 2 - 1, 1)
            sp.wait_ge(rows_stored, 16 * E)

        def pairs_of_experts(eng, expert):
            for i in range(2):
                expert(0, i, i)
            with eng.Fori(1, E // 2) as g:
                for i in range(2):
                    expert(g, i, 2 * g + i)

        @block.tensor
        def _(pe):
            def expert(g, i, e):
                pe.wait_ge(loaded[i], PER * g + PER)
                for k in range(KC):
                    for t in range(ST):
                        mm = pe.transpose(ps_t[k][:, t * P:t * P + P], slots[i][:, t, k * P:k * P + P], ident)
                    mm.then_inc(t_full, 1)
                pe.wait_ge(t_ready, KC * e + KC)
                for f in range(IT):
                    wait(pe, h_ready, IT * e + f - 1)
                    for k in range(KC):
                        mm = pe.matmul(ps_h[f % 2][:, :], wi[i][:, k, f * P:f * P + P], slots_t[:, k, :],
                                       start=(k == 0), stop=(k == KC - 1))
                    mm.then_inc(h_full, 1)
                pe.wait_ge(h_ready, IT * e + IT)
                for v in range(ST // 2):
                    wait(pe, o_ready, 2 * e + v - 1)
                    for u in (2 * v, 2 * v + 1):
                        for f in range(IT):
                            mm = pe.matmul(ps_o[v][:, (u % 2) * C:(u % 2) * C + C], hidden[:, f, u * P:u * P + P],
                                           wo[i][:, f, :], start=(f == 0), stop=(f == IT - 1))
                    mm.then_inc(o_full, 1)
            pairs_of_experts(pe, expert)

        @block.scalar
        def _(act):
            def expert(g, i, e):
                for f in range(IT):
                    act.wait_ge(h_full, IT * e + f + 1)
                    act.activation(hidden[:, f, :], ps_h[f % 2][:, :], ACT.Gelu).then_inc(h_ready, 1)
            pairs_of_experts(act, expert)

        @block.vector
        def _(dve):
            def expert(g, i, e):
                for k in range(KC):
                    dve.wait_ge(t_full, KC * e + k + 1)
                    dve.tensor_copy(slots_t[:, k, :], ps_t[k][:, :]).then_inc(t_ready, 1)
                for v in range(ST // 2):
                    dve.wait_ge(o_full, 2 * e + v + 1)
                    wait(dve, rows_stored, 16 * e)
                    dve.tensor_copy(rows[:, 2 * v:2 * v + 2, :],
                                    ps_o[v][:, :].rearrange("p (t c) -> p t c", t=2)).then_inc(o_ready, 1)
            pairs_of_experts(dve, expert)


def combine(nc, io, weight, gather_at, half_pow, x2_dram, rows_dram):
    R = 4
    with ExitStack() as ctx:
        def sb(name, shape, dt=F32):
            return ctx.enter_context(nc.sbuf_tensor(name, shape, dt))

        def sem(name):
            return ctx.enter_context(nc.semaphore(name))

        at = sb("at", [P, R, TT], I32)
        w = sb("w", [P, R, TT])
        got = sb("got", [P, R, TT, C])
        base = sb("base", [P, R, TT, C])
        y = sb("y", [P, R, TT, C])
        res = sb("res", [P, R, TT, C])
        st = sb("st", [P, R, TT, 6])
        m = sb("m", [P, R, TT, 2])
        var = sb("var", [P, R, TT])
        root = sb("root", [P, R, TT])
        at_ready, w_ready = sem("at_ready"), sem("w_ready")
        gathered = [sem(f"gathered{i}") for i in range(R)]
        base_in = [sem(f"base_in{i}") for i in range(R)]
        stored = [sem(f"stored{i}") for i in range(R)]
        y_ready, var_done, root_done, res_ready = sem("y_ready"), sem("var_done"), sem("root_done"), sem("res_ready")
        steps, stood, c_sp_stood, c_pool_stood = (
            sem("c_steps"), sem("c_stood"), sem("c_sp_stood"), sem("c_pool_stood"))
        STEPS_C = 2

        block = ctx.enter_context(nc.Block())

        def rings(eng, batch):
            for i in range(R):
                batch(0, i, i)
            with eng.Fori(1, B // R) as g:
                for i in range(R):
                    batch(g, i, g * R + i)

        @block.sync
        def _(sp):
            def load(g, i, b):
                wait(sp, y_ready, b - R + 1)
                stand(sp, c_sp_stood)
                sp.dma_start(base[:, i, :, :], batch_of(x2_dram, b)).then_inc(base_in[i], 16)

            def store(g, i, b):
                sp.wait_ge(res_ready, b + 1)
                stand(sp, c_sp_stood)
                sp.dma_start(batch_of(io["out"], b), res[:, i, :, :]).then_inc(stored[i], 16)

            for i in range(R):
                load(0, i, i)
            with sp.Fori(1, B // R) as g:
                for i in range(R):
                    load(g, i, g * R + i)
                    store(g - 1, i, g * R + i - R)
            for i in range(R):
                store(B // R - 1, i, B - R + i)
            for i in range(R):
                sp.wait_ge(stored[i], 16 * (B // R))

        @block.gpsimd
        def _(pool):
            last_slot = pool.to_reg(E * CAP - 1)

            def gather(g, i, b):
                pool.wait_ge(at_ready, b + 1)
                wait(pool, y_ready, b - R + 1)
                stand(pool, c_pool_stood)
                for t in range(TT):
                    pool.indirect_dma_start(
                        out=got[:, i, t, :], out_offset=None, in_=rows_dram,
                        in_offset=bass.IndirectOffsetOnAxis(ap=at[:, i, t:t + 1], axis=0),
                        bounds_check=last_slot, oob_is_err=False).then_inc(gathered[i], 16)

            def power(i, b):
                pool.wait_ge(var_done, b + 1)
                pool.tensor_tensor(root[:, i, :], var[:, i, :], half_pow[:, :], ALU.pow).then_inc(root_done, 1)

            gather(0, 0, 0)
            gather(0, 1, 1)
            for i in range(2, R):
                gather(0, i, i)
                power(i - 2, i - 2)
            with pool.Fori(1, B // R) as g:
                for i in range(R):
                    gather(g, i, g * R + i)
                    power((i - 2) % R, g * R + i - 2)
            for b in (B - 2, B - 1):
                power(b % R, b)

        @block.vector
        def _(dve):
            def pick(g, i, b):
                if not is_zero(g):
                    dve.wait_ge(gathered[i], 32 * g)
                dve.tensor_copy(at[:, i, :], gather_at[:, bass.ds(b * TT, TT)]).then_inc(at_ready, 1)

            def front(g, i, b):
                dve.tensor_scalar(w[:, i, :], weight[:, bass.ds(b * TT, TT)], 0.5, None, ALU.mult).then_inc(w_ready, 1)
                dve.wait_ge(w_ready, b + 1)
                dve.wait_ge(gathered[i], 32 * g + 32)
                dve.wait_ge(base_in[i], 16 * g + 16)
                for t in range(TT):
                    last = dve.scalar_tensor_tensor(out=y[:, i, t, :], in0=got[:, i, t, :], scalar=w[:, i, t:t + 1],
                                                    in1=base[:, i, t, :], op0=ALU.mult, op1=ALU.add)
                last.then_inc(y_ready, 1)
                dve.wait_ge(y_ready, b + 1)
                for t in range(TT):
                    last = dve.bn_stats(st[:, i, t, :], y[:, i, t, :])
                last.then_inc(steps, 1)
                dve.wait_ge(steps, STEPS_C * b + 1)
                stand(dve, stood)
                for t in range(TT):
                    last = dve.bn_aggr(m[:, i, t, :], st[:, i, t, :])
                last.then_inc(steps, 1)
                dve.wait_ge(steps, STEPS_C * b + 2)
                dve.tensor_scalar(var[:, i, :], m[:, i, :, 1], EPS_LN / 4, None, ALU.add).then_inc(var_done, 1)

            def back(g, i, b):
                dve.wait_ge(root_done, b + 1)
                wait(dve, stored[i], 16 * g)
                for t in range(TT):
                    last = dve.tensor_scalar(res[:, i, t, :], y[:, i, t, :], m[:, i, t, 0:1], root[:, i, t:t + 1],
                                             ALU.subtract, ALU.mult)
                last.then_inc(res_ready, 1)

            for i in range(R):
                pick(0, i, i)
            for i in range(R):
                front(0, i, i)
                if i >= 2:
                    back(0, i - 2, i - 2)
            with dve.Fori(1, B // R) as g:
                for i in range(R):
                    pick(g, i, g * R + i)
                for i in range(R):
                    front(g, i, g * R + i)
                    back(g if i >= 2 else g - 1, (i - 2) % R, g * R + i - 2)
            for i in (R - 2, R - 1):
                back(B // R - 1, i, B - R + i)


def _layout(a):
    import numpy as np

    f = {k: np.asarray(v) for k, v in a.items()}

    def channels_first(w):
        return w.T.reshape(-1, P, w.shape[0]).transpose(1, 0, 2)

    def batch_channels_first(v):
        return v.transpose(0, 2, 1).reshape(v.shape[0], KC, P, v.shape[1]).transpose(0, 2, 1, 3)

    def on_all_partitions(*rows):
        return np.broadcast_to(np.stack(rows)[None], (P, len(rows), rows[0].shape[0]))

    head = np.arange(P) // LD
    consts = np.concatenate([
        np.eye(P), np.triu(np.ones((P, P)), 1), np.ones((P, P)),
        head[:, None] == head[None], head[:, None] == np.arange(HP)[None],
        np.broadcast_to(np.arange(E)[None], (P, E))], axis=1).astype(np.float32)
    x = f["x"]
    mask = f["mask_Bx16xSxS_bk1"]
    out = {
        "consts": consts,
        "x": x.reshape(B, TT, P, C).transpose(0, 2, 1, 3),
        "x_t": batch_channels_first(x),
        "f_t": np.concatenate([batch_channels_first(f["fside_BxSxS_0"]), batch_channels_first(f["ctx_1024"])], axis=3),
        "mask": mask.reshape(B, XH, TT, P, S).transpose(0, 3, 1, 2, 4).reshape(B, P, STEPS, S),
        "wqkv": channels_first(f["L0_attn_Wqkv"]),
        "wproj": channels_first(f["L0_attn_Wproj"]),
        "wq": channels_first(f["L0_xattn_Wq"]),
        "wk": channels_first(f["L0_xattn_Wk"]),
        "wgk": channels_first(f["L0_xattn_Wgk"]),
        "wv": channels_first(f["L0_xattn_Wv"]),
        "wgv": channels_first(f["L0_xattn_Wgv"]),
        "wo": channels_first(f["L0_xattn_Wo"]),
        "wgate": channels_first(f["L0_ffn_gate_weight"]),
        "col_bias": np.stack([f["L0_xattn_bq"], f["L0_xattn_bk"], f["L0_xattn_bgk"]]).reshape(3, PAIRS, P).transpose(2, 0, 1),
        "row_bias": on_all_partitions(f["L0_attn_bproj"], f["L0_xattn_bo"], f["L0_ffn_ln_gamma"], f["L0_ffn_ln_beta"]),
        "v_bias": on_all_partitions(f["L0_xattn_bv"], f["L0_xattn_bgv"]),
        "wi": f["L0_ffn_wi"].reshape(E, KC, P, I).transpose(0, 2, 1, 3),
        "wo_e": f["L0_ffn_wo"].reshape(E, IT, P, C).transpose(0, 2, 1, 3),
    }
    return {k: np.ascontiguousarray(v) for k, v in out.items()}


def kernel(**inputs):
    import numpy as np
    import concourse.bacc as bacc
    from concourse.bass_utils import run_bass_kernel_spmd

    arrays = _layout(inputs)
    nc = bacc.Bacc("TRN2", target_bir_lowering=False, num_devices=1)
    io = {name: nc.dram_tensor("in_" + name, a.shape, mybir.dt.from_np(a.dtype), kind="ExternalInput").ap()
          for name, a in arrays.items()}
    io["out"] = nc.dram_tensor("out", (B, P, TT, C), F32, kind="ExternalOutput").ap()
    decoder_kernel(nc, io)
    r = run_bass_kernel_spmd(nc, [{"in_" + name: a for name, a in arrays.items()}], core_ids=[0])
    out = r.results[0]["out"]
    return np.ascontiguousarray(out.transpose(0, 2, 1, 3)).reshape(B, S, C)
```

```python
from contextlib import ExitStack

import concourse.bass as bass
from concourse import mybir

ALU = mybir.AluOpType
ACT = mybir.ActivationFunctionType
AX = mybir.AxisListType
F32 = mybir.dt.float32
BF16 = mybir.dt.bfloat16
U8 = mybir.dt.uint8
F32R = mybir.dt.float32r
I32 = mybir.dt.int32
U32 = mybir.dt.uint32

P = 128
B, S, C = 32, 256, 256
TT = S // P
KC = C // P
LH, LD = 16, 16
HP = P // LD
XH, DK = 16, 64
XF = XH * DK
PAIRS = XH // 2
G = 77
NK = S + G
KT_TILES = (P, P, G)
PW = 3 * P
STEPS = XH * TT
E, I = 8, 1024
CAP = 512
ST = CAP // P
IT = I // P
TILES = B * TT
EPS_LIN = 1e-6
EPS_LN = 1e-5
MASKED = -1e30
SCALE = DK ** -0.5
NL = LD * HP + HP

NKP = NK + 1
RING = 2

ROUTER = ["tok_t0", "tok_t1", "logits", "rank"]
OWN = ["lin_q0", "lin_q1", "lin_kv0", "lin_kv1", "v0", "lin_sum", "v1", "tok_t0", "tok_t1", "lin_out0", "lin_out1",
       "v2", "logits", "lin_t", "v3", "rank", "lin_proj", "k0", "v4", "x1_t", "k1", "q0", "v5"]
for _s in range(1, 4 * PAIRS + 8):
    if _s % 4 == 0 and _s // 4 + 1 < PAIRS:
        OWN.append(f"k{_s // 4 + 1}")
    if _s % 4 == 1 and _s // 4 + 1 < PAIRS:
        OWN.append(f"q{_s // 4 + 1}")
    if _s % 4 == 1 and 0 <= (_s - 9) // 4 < PAIRS:
        OWN.append(f"o_t{(_s - 9) // 4}")
FILLS = [n for n in OWN if n not in ROUTER], OWN, ROUTER
assert all(len(f) % 2 == 0 for f in FILLS)

CHAIN = 10 + PAIRS
ROUTER_CHAIN = 17
ROUNDED = [n for n in OWN if n == "x1_t" or n[0] in "kq" or n[:3] == "o_t"]


def wait(eng, sem, value):
    if not isinstance(value, int) or value > 0:
        eng.wait_ge(sem, value)


def stand(eng, sem):
    eng.sem_inc(sem, 1)


def gen_at(b, name):
    first, other, last = FILLS
    if is_zero(b):
        before, fills = 0, first
    else:
        before, fills = (len(first) - len(other)) // 2 + b * (len(other) // 2), last if isinstance(b, int) and b == B else other
    n = fills.index(name)
    return n % 2, before + n // 2 + 1


def rounded_at(b, name):
    return b * len(ROUNDED) + ROUNDED.index(name) + 1


def chain(eng, sem, b, per_batch):
    done = [0]

    def link(ins):
        done[0] += 1
        assert done[0] <= per_batch
        ins.then_inc(sem, 1)
        eng.wait_ge(sem, b * per_batch + done[0])
    return link, done


def decoder_kernel(nc, io):
    with ExitStack() as keep:
        def dram(name, shape):
            return nc.dram_tensor(name, shape, F32, kind="Internal").ap()

        x2_dram = dram("x2_dram", [B, P, TT, C])
        slots_dram = dram("slots_dram", [E * CAP, C])
        rows_dram = dram("rows_dram", [E * CAP, C])

        consts = keep.enter_context(nc.sbuf_tensor("consts", [P, 3 * P + NL + E], F32))
        weight = keep.enter_context(nc.sbuf_tensor("weight", [P, TILES], F32))
        gather_at = keep.enter_context(nc.sbuf_tensor("gather_at", [P, TILES], I32))
        half_pow = keep.enter_context(nc.sbuf_tensor("half_pow", [P, TT], F32))
        attention_and_router(nc, io, consts, weight, gather_at, half_pow, x2_dram, slots_dram)
        experts(nc, io, consts, slots_dram, rows_dram)
        combine(nc, io, weight, gather_at, half_pow, x2_dram, rows_dram)


def attention_and_router(nc, io, consts, weight, gather_at, half_pow, x2_dram, slots_dram):
    with ExitStack() as ctx:
        def sb(name, shape, dt=F32):
            return ctx.enter_context(nc.sbuf_tensor(name, shape, dt))

        def split(name, shape):
            return sb(name + "_hi", shape, F32R), sb(name + "_lo", shape, F32R)

        def sem(name):
            return ctx.enter_context(nc.semaphore(name))

        def bank(name):
            return ctx.enter_context(nc.psum_tensor(name, [P, 512], F32))

        ident = consts[:, 0:P]
        before = consts[:, P:2 * P]
        ones = consts[:, 2 * P:3 * P]
        own_head = consts[:, 3 * P:3 * P + NL]
        expert_no = consts[:, 3 * P + NL:3 * P + NL + E]

        wqkv = split("wqkv", [P, KC, 3 * C])
        wproj = sb("wproj", [P, KC, C])
        wq = split("wq", [P, KC, XF])
        wk = split("wk", [P, KC, XF])
        wgk = sb("wgk", [P, KC, XF])
        wv = split("wv", [P, KC, XF])
        wgv = sb("wgv", [P, KC, XF])
        wo = split("wo", [P, PAIRS, C])
        wgate = sb("wgate", [P, KC, E])
        col_bias = sb("col_bias", [P, 3, PAIRS])
        row_bias = sb("row_bias", [P, 4, C])
        v_bias = sb("v_bias", [P, 2, XF])
        x_t_in = sb("x_t_in", [P, KC, S])
        x_t = split("x_t", [P, KC, S])
        x_in = sb("x_in", [P, TT, C])
        f_t_in = sb("f_t_in", [P, KC, NK])
        f_t = split("f_t", [P, KC, S])
        mask_in = sb("mask_in", [P, 2, STEPS // 4, S], U8)
        mask_add = sb("mask_add", [P, 4 * RING, NKP], BF16)
        e_x = sb("e_x", [P, 4, C])
        lin_q = sb("lin_q", [P, KC, S])
        lin_k = sb("lin_k", [P, TT, C])
        lin_v = sb("lin_v", [P, TT, KC, NL])
        lin_kv = sb("lin_kv", [P, KC, NL])
        lin_den = sb("lin_den", [P, TT, KC, HP])
        lin_at = sb("lin_at", [P, KC, S])
        z = sb("z", [P, TT, C])
        lin_a = z
        stats = sb("stats", [P, TT, 6])
        mv = sb("mv", [P, TT, 2])
        var_eps = sb("var_eps", [P, TT])
        rstd = sb("rstd", [P, TT])
        x1 = sb("x1", [P, TT, C])
        x1_t = split("x1_t", [P, KC, S])
        q_z = split("q_z", [P, 2 * RING, S])
        k_t = split("k_t", [P, RING, NKP])
        v_s = sb("v_s", [P, 3, XF])
        masked = sb("masked", [P, 2, NKP])
        low = sb("low", [P, STEPS])
        prob = sb("prob", [P, 3, PW])
        total = sb("total", [P, STEPS])
        inv_total = sb("inv_total", [P, 4])
        prob_t = sb("prob_t", [P, 2, PW])
        o_s = sb("o_s", [P, 2, TT, P])
        o_t = split("o_t", [P, 2, S])
        x2 = sb("x2", [P, TT, C])
        tok = sb("tok", [P, TT, C])
        tok_t = sb("tok_t", [P, KC, S])
        r_stats = sb("r_stats", [P, TT, 6])
        r_mv = sb("r_mv", [P, TT, 2])
        r_var = sb("r_var", [P, TT])
        r_rstd = sb("r_rstd", [P, TT])
        logit = sb("logit", [P, TT, E])
        top = sb("top", [P, TT, 8])
        top_at = sb("top_at", [P, TT, 8], U32)
        top_f = sb("top_f", [P, TT])
        rel = sb("rel", [P, TT, E])
        e_rel = sb("e_rel", [P, TT, E])
        e_sum = sb("e_sum", [P, TT])
        p_top = sb("p_top", [P, TT])
        onehot = sb("onehot", [P, TT, E])
        seen = sb("seen", [P, TT, E])
        own_rank = sb("own_rank", [P, TT, E])
        rank = sb("rank", [P, TT])
        kept_rank = sb("kept_rank", [P, TT])
        beyond = sb("beyond", [P, TT])
        slot_f = sb("slot_f", [P, TT])
        scatter_at = sb("scatter_at", [P, TT], I32)

        gen = [bank("gen0"), bank("gen1")]
        score = [bank("score0"), bank("score1")]
        prt = [bank("prt0"), bank("prt1")]
        out_ps = bank("out_ps")
        o_proj = bank("o_proj")

        consts_loaded, weights_loaded = sem("consts_loaded"), sem("weights_loaded")
        x_t_loaded, x_loaded, f_t_loaded = sem("x_t_loaded"), sem("x_loaded"), sem("f_t_loaded")
        mask_loaded = [sem(f"mask_loaded{i}") for i in range(2)]
        staged = [sem(f"staged{i}") for i in range(3)]
        stage_rounded, stage_split = sem("stage_rounded"), sem("stage_split")
        x_split, f_split, f_rounded = sem("x_split"), sem("f_split"), sem("f_rounded")
        x_rounded = sem("x_rounded")
        slots_zeroed, scattered, scatter_done = sem("slots_zeroed"), sem("scattered"), sem("scatter_done")
        x2_stored, x2_free = sem("x2_stored"), sem("x2_free")
        pool_zeros, dve_zeros = sem("pool_zeros"), sem("dve_zeros")
        gen_full = [sem("gen_full0"), sem("gen_full1")]
        gen_free = [sem("gen_free0"), sem("gen_free1")]
        o_proj_full, o_proj_free = sem("o_proj_full"), sem("o_proj_free")
        rounded = sem("rounded")
        score_full, prt_full, out_full = sem("score_full"), sem("prt_full"), sem("out_full")
        exp_ready, lin_v_ready = sem("exp_ready"), sem("lin_v_ready")
        lin_a_ready = sem("lin_a_ready")
        x_bias_ready, x1_bias_ready = sem("x_bias_ready"), sem("x1_bias_ready")
        var_ready, rstd_ready = sem("var_ready"), sem("rstd_ready")
        x1_ready, x2_ready = sem("x1_ready"), sem("x2_ready")
        mask_ready, masked_ready = sem("mask_ready"), sem("masked_ready")
        prob_ready, prob_t_ready, o_ready = sem("prob_ready"), sem("prob_t_ready"), sem("o_ready")
        normed_ready, tok_ready = sem("normed_ready"), sem("tok_ready")
        r_var_ready, r_rstd_ready = sem("r_var_ready"), sem("r_rstd_ready")
        rel_ready, e_rel_ready = sem("rel_ready"), sem("e_rel_ready")
        seen_ready, scatter_ready = sem("seen_ready"), sem("scatter_ready")
        dve_chain, dve_router_chain = sem("dve_chain"), sem("dve_router_chain")
        affine_half = sem("affine_half")
        dve_stood, pool_stood, sp_stood = sem("dve_stood"), sem("pool_stood"), sem("sp_stood")

        block = ctx.enter_context(nc.Block())

        stages = []
        for w, name in ((wqkv, "wqkv"), (wv, "wv"), (wk, "wk"), (wq, "wq")):
            stages += [(io[name][:, k, :], [h[:, k, :] for h in w]) for k in range(KC)]
        stages += [(io["wo"][:, k * 4:k * 4 + 4, :].rearrange("p j c -> p (j c)"),
                    [h[:, k * 4:k * 4 + 4, :].rearrange("p j c -> p (j c)") for h in wo]) for k in range(KC)]
        whole = ((wproj, "wproj"), (wgk, "wgk"), (wgv, "wgv"), (wgate, "wgate"), (col_bias, "col_bias"),
                 (row_bias, "row_bias"), (v_bias, "v_bias"))
        ZEROED = E * CAP // (P * TT)

        @block.sync
        def _(sp):
            def load_x_t(b):
                wait(sp, x_split, b)
                stand(sp, sp_stood)
                sp.dma_start(x_t_in[:, :, :], batch_of(io["x_t"], b)).then_inc(x_t_loaded, 16)

            def load_x(b):
                if not is_zero(b):
                    k, n = gen_at(b - 1, "lin_proj")
                    sp.wait_ge(gen_free[k], n)
                stand(sp, sp_stood)
                sp.dma_start(x_in[:, :, :], batch_of(io["x"], b)).then_inc(x_loaded, 16)

            def load_f_t(b):
                if not is_zero(b):
                    k, n = gen_at(b - 1, f"k{PAIRS - 1}")
                    sp.wait_ge(gen_free[k], n)
                stand(sp, sp_stood)
                sp.dma_start(f_t_in[:, :, :], batch_of(io["f_t"], b)).then_inc(f_t_loaded, 16)

            def load_mask(b, u):
                wait(sp, mask_ready, PAIRS * b + 2 * u - 2)
                stand(sp, sp_stood)
                n = STEPS // 4
                sp.dma_start(mask_in[:, u % 2, :, :], batch_of(io["mask"], b, slice(u * n, u * n + n))
                             ).then_inc(mask_loaded[u % 2], 16)

            def store(b):
                sp.wait_ge(x2_ready, b + 1)
                stand(sp, sp_stood)
                sp.dma_start(batch_of(x2_dram, b), x2[:, :, :]).then_inc(x2_stored, 16)

            def batch(b, last=False):
                if not last:
                    load_x_t(b + 1)
                if not is_zero(b):
                    store(b - 1)
                if not last:
                    load_x(b + 1)
                load_mask(b, 2)
                load_mask(b, 3)
                if not is_zero(b):
                    sp.wait_ge(x2_stored, 16 * b)
                sp.sem_inc(x2_free, 1)
                if not last:
                    load_mask(b + 1, 0)
                    load_mask(b + 1, 1)
                    load_f_t(b + 1)

            load_x_t(0)
            load_f_t(0)
            sp.dma_start(consts[:, :], io["consts"]).then_inc(consts_loaded, 16)
            for n, (src, halves) in enumerate(stages):
                wait(sp, stage_split, n - 2)
                sp.dma_start(v_s[:, n % 3, 0:src.shape[-1]], src).then_inc(staged[n % 3], 16)
            for dst, name in whole:
                sp.dma_start(dst[:, :, :], io[name]).then_inc(weights_loaded, 16)
            load_x(0)
            load_mask(0, 0)
            load_mask(0, 1)
            sp.wait_ge(pool_zeros, 1)
            slot_rows = slots_dram.rearrange("(n p t) c -> n p (t c)", p=P, t=TT)
            for n in range(ZEROED):
                sp.dma_start(slot_rows[n], tok[:, :, :].rearrange("p t c -> p (t c)")).then_inc(slots_zeroed, 16)
            batch(0)
            with sp.Fori(1, B - 1) as b:
                batch(b)
            batch(B - 1, last=True)
            store(B - 1)
            sp.wait_ge(slots_zeroed, 16 * ZEROED)
            sp.wait_ge(x2_stored, 16 * B)

        @block.tensor
        def _(pe):
            def multiply(out, lhs, rhs, tiles, first=True, last=True, **how):
                if isinstance(lhs, tuple):
                    terms = [(lhs[0], rhs[0]), (lhs[0], rhs[1]), (lhs[1], rhs[0])]
                else:
                    terms = [(lhs, rhs)]
                n = len(terms) * tiles
                for k in range(tiles):
                    for i, (x, y) in enumerate(terms):
                        at = k * len(terms) + i
                        mm = pe.matmul(out, x[:, k], y[:, k], start=first and at == 0, stop=last and at == n - 1, **how)
                return mm

            def part(x, *index):
                if isinstance(x, tuple):
                    return tuple(h[(slice(None), slice(None)) + index] for h in x)
                return x[(slice(None), slice(None)) + index]

            def fill(b, name):
                k, n = gen_at(b, name)
                wait(pe, gen_free[k], n - 1)
                return gen[k], gen_full[k]

            def read(b, name):
                k, n = gen_at(b, name)
                pe.wait_ge(gen_free[k], n)

            def project(b, name, parts):
                ps, full = fill(b, name)
                for (c0, c1), lhs, rhs in parts:
                    m = (lhs[0] if isinstance(lhs, tuple) else lhs).shape[-1]
                    mm = multiply(ps[0:m, c0:c1], lhs, rhs, KC)
                mm.then_inc(full, 1)

            def keys(b, j):
                f = slice(j * P, j * P + P)
                project(b, f"k{j}", [((0, S), part(wk, f), f_t), ((S, NK), wgk[:, :, f], f_t_in[:, :, S:NK])])

            def queries(b, j):
                project(b, f"q{j}", [((0, S), part(wq, slice(j * P, j * P + P)), x1_t)])

            def values(b, n):
                t, half = n // 2, n % 2
                f = slice(half * 512, half * 512 + 512)
                if t < 2:
                    project(b, f"v{n}", [((0, 512), part(f_t, slice(t * P, t * P + P)), part(wv, f))])
                else:
                    project(b, f"v{n}", [((0, 512), f_t_in[:, :, S:NK], wgv[:, :, f])])

            def transposes(b, src, name, tiles=range(KC)):
                ps, full = fill(b, name)
                blocks = [(k, t) for k in tiles for t in range(TT)]
                for n, (k, t) in enumerate(blocks):
                    mm = pe.transpose(ps[:, n * P:n * P + P], src[:, t, k * P:k * P + P], ident)
                mm.then_inc(full, 1)

            def router_tokens(r):
                pe.wait_ge(tok_ready, r + 1)
                for k in range(KC):
                    transposes(r + 1, tok, f"tok_t{k}", [k])

            def router_logits(r):
                ps, full = fill(r + 1, "logits")
                for k in range(KC):
                    read(r + 1, f"tok_t{k}")
                for t in range(TT):
                    mm = multiply(ps[:, t * E:t * E + E], tok_t[:, :, t * P:t * P + P], wgate, KC)
                mm.then_inc(full, 1)

            def router_rank(r):
                ps, full = fill(r + 1, "rank")
                pe.wait_ge(seen_ready, r + 1)
                pe.matmul(ps[:, 0:TT * E], before, onehot[:, :, :], start=True, stop=False)
                pe.matmul(ps[:, 0:TT * E], ones, seen[:, :, :], start=False, stop=True).then_inc(full, 1)

            def output(b, j):
                if j == 0:
                    wait(pe, o_proj_free, b)
                read(b, f"o_t{j}")
                for t in range(TT):
                    mm = multiply(o_proj[:, t * C:t * C + C],
                                  tuple(o[:, j % 2:j % 2 + 1, t * P:t * P + P] for o in o_t),
                                  tuple(w[:, j:j + 1, :] for w in wo), 1, first=(j == 0 and t == 0),
                                  last=(j == PAIRS - 1), skip_group_check=True)
                if j == PAIRS - 1:
                    mm.then_inc(o_proj_full, 1)

            def attend(b):
                for s in range(STEPS + 10):
                    j = s // 4
                    if s < STEPS:
                        h, t = s // TT, s % TT
                        if s % 4 == 0:
                            read(b, f"k{j}")
                            read(b, f"q{j}")
                        wait(pe, masked_ready, STEPS * b + s - 1)
                        slot = h % (2 * RING)
                        multiply(score[s % 2][:, 0:NKP], tuple(q[:, slot:slot + 1, t * P:t * P + P] for q in q_z),
                                 tuple(k[:, j % RING:j % RING + 1, :] for k in k_t), 1).then_inc(score_full, 1)
                    if s >= 4 and s % 4 == 0 and j + 1 < PAIRS:
                        keys(b, j + 1)
                    if s % 4 == 1 and j + 1 < PAIRS:
                        queries(b, j + 1)
                    n = s - 2
                    if 0 <= n < STEPS:
                        wait(pe, prob_t_ready, STEPS * b + n - 1)
                        pe.wait_ge(prob_ready, STEPS * b + n + 1)
                        for k in range(3):
                            mm = pe.transpose(prt[n % 2][:, k * P:k * P + P], prob[:, n % 3, k * P:k * P + P], ident)
                        mm.then_inc(prt_full, 1)
                    n = s - 4
                    if 0 <= n < STEPS:
                        h, c = n // TT, n % 4
                        if n == 0:
                            read(b, "v4")
                            read(b, "v5")
                        if c == 0:
                            wait(pe, o_ready, PAIRS * b + n // 4)
                        pe.wait_ge(prob_t_ready, STEPS * b + n + 1)
                        for k in range(3):
                            rows = KT_TILES[k]
                            mm = pe.matmul(out_ps[:, c * DK:c * DK + DK], prob_t[0:rows, n % 2, k * P:k * P + P],
                                           v_s[0:rows, k, h * DK:h * DK + DK], start=(k == 0), stop=(k == 2))
                        mm.then_inc(out_full, 1)
                    j, r = divmod(s - 9, 4)
                    if 0 <= j < PAIRS and r == 0:
                        ps, full = fill(b, f"o_t{j}")
                        pe.wait_ge(o_ready, PAIRS * b + j + 1)
                        for t in range(TT):
                            mm = pe.transpose(ps[:, t * P:t * P + P], o_s[:, j % 2, t, :], ident)
                        mm.then_inc(full, 1)
                    j, r = divmod(s - 11, 4)
                    if 0 <= j < PAIRS - 1 and r == 0:
                        output(b, j)

            def batch(b):
                router = not is_zero(b)
                pe.wait_ge(x_split, b + 1)
                for k in range(KC):
                    project(b, f"lin_q{k}", [((0, S), part(wqkv, slice(k * P, k * P + P)), x_t)])
                if router:
                    output(b - 1, PAIRS - 1)
                for t in range(TT):
                    project(b, f"lin_kv{t}", [((0, 512), part(x_t, slice(t * P, t * P + P)), part(wqkv, slice(C, 3 * C)))])
                pe.wait_ge(f_split, b + 1)
                values(b, 0)
                ps, full = fill(b, "lin_sum")
                read(b, "lin_kv0")
                read(b, "lin_kv1")
                for k in range(KC):
                    for t in range(TT):
                        mm = pe.matmul(ps[:, k * NL:k * NL + NL], lin_k[:, t, k * P:k * P + P], lin_v[:, t, k, :],
                                       start=(t == 0), stop=(t == TT - 1))
                mm.then_inc(full, 1)
                values(b, 1)
                if router:
                    router_tokens(b - 1)
                read(b, "lin_sum")
                for t in range(TT):
                    ps, full = fill(b, f"lin_out{t}")
                    for k in range(KC):
                        mm = pe.matmul(ps[:, k * NL:k * NL + NL], lin_q[:, k, t * P:t * P + P], lin_kv[:, k, :],
                                       start=True, stop=True)
                    mm.then_inc(full, 1)
                values(b, 2)
                if router:
                    router_logits(b - 1)
                pe.wait_ge(lin_a_ready, TT * b + TT)
                transposes(b, lin_a, "lin_t")
                values(b, 3)
                if router:
                    router_rank(b - 1)
                read(b, "lin_t")
                project(b, "lin_proj", [((t * C, t * C + C), lin_at[:, :, t * P:t * P + P], wproj) for t in range(TT)])
                keys(b, 0)
                values(b, 4)
                pe.wait_ge(x1_ready, b + 1)
                transposes(b, x1, "x1_t")
                keys(b, 1)
                read(b, "x1_t")
                queries(b, 0)
                values(b, 5)
                attend(b)

            pe.wait_ge(consts_loaded, 16)
            pe.wait_ge(weights_loaded, len(whole) * 16)
            pe.wait_ge(stage_split, len(stages))
            pe.wait_ge(pool_zeros, 2)
            pe.wait_ge(dve_zeros, 3)
            batch(0)
            with pe.Fori(1, B) as b:
                batch(b)
            output(B - 1, PAIRS - 1)
            router_tokens(B - 1)
            router_logits(B - 1)
            router_rank(B - 1)

        @block.scalar
        def _(act):
            def own(name, b):
                k, n = gen_at(b, name)
                act.wait_ge(gen_full[k], n)
                return gen[k], gen_free[k]

            def flat(t):
                return t[:, :, :].rearrange("p a b -> p (a b)")

            def keys(b, j):
                ps, _ = own(f"k{j}", b)
                hi = k_t[0]
                act.activation(hi[:, j % RING, 0:S], ps[:, 0:S], ACT.Identity, bias=col_bias[:, 1, j:j + 1])
                act.activation(hi[:, j % RING, S:NK], ps[:, S:NK], ACT.Identity,
                               bias=col_bias[:, 2, j:j + 1]).then_inc(rounded, 1)

            def queries(b, j):
                ps, _ = own(f"q{j}", b)
                for i in range(2):
                    rows = slice(i * DK, i * DK + DK)
                    last = act.activation(q_z[0][rows, 2 * (j % RING) + i, :], ps[rows, 0:S], ACT.Identity,
                                          bias=col_bias[rows, 0, j:j + 1])
                last.then_inc(rounded, 1)

            def router_tokens(r):
                for k in range(KC):
                    ps, free = own(f"tok_t{k}", r + 1)
                    act.activation(tok_t[:, k, :], ps[:, 0:S], ACT.Copy).then_inc(free, 1)

            def router_exp(r):
                act.wait_ge(rel_ready, r + 1)
                act.activation(e_rel[:, :, :], rel[:, :, :], ACT.Exp).then_inc(e_rel_ready, 1)

            def batch(b):
                router = not is_zero(b)
                for k in range(KC):
                    ps, free = own(f"lin_q{k}", b)
                    act.activation(e_x[:, k, :], ps[:, 0:C], ACT.Exp).then_inc(exp_ready, 1)
                for t in range(TT):
                    ps, free = own(f"lin_kv{t}", b)
                    act.activation(lin_v[:, t, :, 0:P], ps[:, C:2 * C].rearrange("p (k c) -> p k c", k=KC), ACT.Copy)
                    act.activation(e_x[:, KC + t, :], ps[:, 0:C], ACT.Exp).then_inc(exp_ready, 1)
                if router:
                    router_tokens(b - 1)
                    router_exp(b - 1)
                ps, free = own("lin_t", b)
                act.activation(flat(lin_at), ps[:, :], ACT.Copy).then_inc(free, 1)
                keys(b, 0)
                ps, _ = own("x1_t", b)
                act.activation(flat(x1_t[0]), ps[:, :], ACT.Copy).then_inc(rounded, 1)
                keys(b, 1)
                queries(b, 0)
                for s in range(STEPS + 10):
                    j = s // 4
                    if s < STEPS:
                        wait(act, prt_full, STEPS * b + s - 2)
                        act.wait_ge(masked_ready, STEPS * b + s + 1)
                        act.activation(prob[:, s % 3, 0:NKP], masked[:, s % 2, :], ACT.Exp, bias=low[:, s:s + 1],
                                       scale=-1.0, accum_out=total[:, s:s + 1]).then_inc(prob_ready, 1)
                    if s >= 4 and s % 4 == 0 and j + 1 < PAIRS:
                        keys(b, j + 1)
                    if s % 4 == 1 and j + 1 < PAIRS:
                        queries(b, j + 1)
                    n = s - 2
                    if 0 <= n < STEPS:
                        wait(act, out_full, STEPS * b + n - 1)
                        act.wait_ge(prt_full, STEPS * b + n + 1)
                        act.activation(prob_t[:, n % 2, :], prt[n % 2][:, 0:PW], ACT.Copy).then_inc(prob_t_ready, 1)
                    j, r = divmod(s - 9, 4)
                    if 0 <= j < PAIRS and r == 0:
                        ps, _ = own(f"o_t{j}", b)
                        act.activation(o_t[0][:, j % 2, :], ps[:, 0:S], ACT.Copy).then_inc(rounded, 1)

            for n, (src, halves) in enumerate(stages):
                act.wait_ge(staged[n % 3], 16 * (n // 3) + 16)
                act.activation(halves[0], v_s[:, n % 3, 0:src.shape[-1]], ACT.Copy).then_inc(stage_rounded, 1)
            act.wait_ge(weights_loaded, len(whole) * 16)
            act.wait_ge(pool_zeros, 2)
            act.wait_ge(dve_zeros, 3)
            batch(0)
            with act.Fori(1, B) as b:
                batch(b)
            router_tokens(B - 1)
            router_exp(B - 1)

        @block.vector
        def _(dve):
            def own(name, b):
                k, n = gen_at(b, name)
                dve.wait_ge(gen_full[k], n)
                return gen[k], gen_free[k]

            def plain(t):
                return t.bitcast(F32)

            def feature(b, n, name, dst, link):
                ps, free = own(name, b)
                dve.wait_ge(exp_ready, 4 * b + n + 1)
                link(dve.tensor_scalar(e_x[:, n, :], e_x[:, n, :], 1.0, None, ALU.min))
                dve.scalar_tensor_tensor(out=dst, in0=ps[:, 0:C], scalar=0.0, in1=e_x[:, n, :],
                                         op0=ALU.max, op1=ALU.add).then_inc(free, 1)

            def moments(src, st, m, var, link, ready):
                for t in range(TT):
                    last = dve.bn_stats(st[:, t, :], src[:, t, :])
                link(last)
                stand(dve, dve_stood)
                for t in range(TT):
                    last = dve.bn_aggr(m[:, t, :], st[:, t, :])
                link(last)
                dve.tensor_scalar(var[:, :], m[:, :, 1], EPS_LN, None, ALU.add).then_inc(ready, 1)

            def normalise(dst, src, m, rs, ready):
                for t in range(TT):
                    last = dve.tensor_scalar(dst[:, t, :], src[:, t, :], m[:, t, 0:1], rs[:, t:t + 1],
                                             ALU.subtract, ALU.mult)
                last.then_inc(ready, 1)

            def router_choice(r, link):
                ps, free = own("logits", r + 1)
                dve.tensor_copy(logit[:, :, :], ps[:, 0:TT * E].rearrange("p (t e) -> p t e", e=E)).then_inc(free, 1)
                k, n = gen_at(r + 1, "logits")
                dve.wait_ge(gen_free[k], n)
                stand(dve, dve_stood)
                for t in range(TT):
                    last = dve.max(top[:, t, :], logit[:, t, :])
                link(last)
                dve.tensor_tensor(rel[:, :, :], logit[:, :, :], top[:, :, 0:1].to_broadcast([P, TT, E]),
                                  ALU.subtract).then_inc(rel_ready, 1)
                for t in range(TT):
                    last = dve.max_index(top_at[:, t, :], top[:, t, :], logit[:, t, :])
                link(last)
                link(dve.tensor_copy(top_f[:, :], top_at[:, :, 0]))
                link(dve.tensor_tensor(onehot[:, :, :], expert_no.unsqueeze(1).to_broadcast([P, TT, E]),
                                       top_f[:, :].unsqueeze(2).to_broadcast([P, TT, E]), ALU.is_equal))
                dve.tensor_tensor(seen[:, 1, :], seen[:, 0, :], onehot[:, 0, :], ALU.add).then_inc(seen_ready, 1)
                dve.wait_ge(e_rel_ready, r + 1)
                link(dve.tensor_reduce(e_sum[:, :], e_rel[:, :, :], AX.X, ALU.add))
                link(dve.reciprocal(p_top[:, :], e_sum[:, :]))

            def router_slots(r, link):
                ps, free = own("rank", r + 1)
                dve.tensor_tensor(own_rank[:, :, :], ps[:, 0:TT * E].rearrange("p (t e) -> p t e", e=E),
                                  onehot[:, :, :], ALU.mult).then_inc(free, 1)
                k, n = gen_at(r + 1, "rank")
                dve.wait_ge(gen_free[k], n)
                link(dve.tensor_reduce(rank[:, :], own_rank[:, :, :], AX.X, ALU.add))
                link(dve.tensor_tensor(seen[:, 0, :], seen[:, 1, :], onehot[:, 1, :], ALU.add))
                link(dve.scalar_tensor_tensor(out=kept_rank[:, :], in0=rank[:, :], scalar=float(CAP), in1=rank[:, :],
                                              op0=ALU.is_lt, op1=ALU.mult))
                link(dve.tensor_scalar(beyond[:, :], rank[:, :], float(CAP), float(2 * E * CAP), ALU.is_ge, ALU.mult))
                link(dve.scalar_tensor_tensor(out=slot_f[:, :], in0=top_f[:, :], scalar=float(CAP), in1=kept_rank[:, :],
                                              op0=ALU.mult, op1=ALU.add))
                dve.wait_ge(scatter_done, r + 1)
                dve.tensor_tensor(scatter_at[:, :], slot_f[:, :], beyond[:, :], ALU.add).then_inc(scatter_ready, 1)
                link(dve.tensor_copy(gather_at[:, bass.ds(r * TT, TT)], slot_f[:, :]))
                link(dve.scalar_tensor_tensor(out=weight[:, bass.ds(r * TT, TT)], in0=rank[:, :], scalar=float(CAP),
                                              in1=p_top[:, :], op0=ALU.is_lt, op1=ALU.mult))

            def values(b, n):
                t, half = n // 2, n % 2
                rows = KT_TILES[t]
                cols = slice(half * 512, half * 512 + 512)
                ps, free = own(f"v{n}", b)
                dve.tensor_tensor(v_s[0:rows, t, cols], ps[0:rows, :], v_bias[0:rows, t // 2, cols],
                                  ALU.add).then_inc(free, 1)

            def keys(b, j):
                ps, free = own(f"k{j}", b)
                dve.wait_ge(rounded, rounded_at(b, f"k{j}"))
                hi, lo = k_t
                for n, cols in ((1, slice(0, S)), (2, slice(S, NK))):
                    last = dve.scalar_tensor_tensor(
                        out=lo[:, j % RING, cols], in0=ps[:, cols], scalar=col_bias[:, n, j:j + 1],
                        in1=plain(hi[:, j % RING, cols]), op0=ALU.add, op1=ALU.subtract)
                last.then_inc(free, 1)

            def queries(b, j):
                ps, free = own(f"q{j}", b)
                dve.wait_ge(rounded, rounded_at(b, f"q{j}"))
                hi, lo = q_z
                for i in range(2):
                    rows = slice(i * DK, i * DK + DK)
                    slot = 2 * (j % RING) + i
                    last = dve.scalar_tensor_tensor(
                        out=lo[rows, slot, :], in0=ps[rows, 0:S], scalar=col_bias[rows, 0, j:j + 1],
                        in1=plain(hi[rows, slot, :]), op0=ALU.add, op1=ALU.subtract)
                last.then_inc(free, 1)

            def rest(b, name, hi, lo, cols):
                ps, free = own(name, b)
                dve.wait_ge(rounded, rounded_at(b, name))
                dve.tensor_tensor(lo, ps[:, 0:cols], plain(hi), ALU.subtract).then_inc(free, 1)

            def residual(r, link):
                dve.wait_ge(x1_bias_ready, r + 1)
                dve.wait_ge(o_proj_full, r + 1)
                dve.tensor_tensor(z[:, :, :], o_proj[:, :].rearrange("p (t c) -> p t c", t=TT), x1[:, :, :],
                                  ALU.add).then_inc(o_proj_free, 1)
                dve.wait_ge(o_proj_free, r + 1)
                moments(z, stats, mv, var_eps, link, var_ready)

            def attended(r, link):
                dve.wait_ge(x2_free, r + 1)
                dve.wait_ge(rstd_ready, 2 * r + 2)
                normalise(x2, z, mv, rstd, x2_ready)
                dve.wait_ge(x2_ready, r + 1)
                moments(x2, r_stats, r_mv, r_var, link, r_var_ready)

            def tokens(r):
                dve.wait_ge(scatter_done, r + 1)
                dve.wait_ge(r_rstd_ready, r + 1)
                normalise(tok, x2, r_mv, r_rstd, normed_ready)

            def batch(b):
                router = not is_zero(b)
                link, done = chain(dve, dve_chain, b, CHAIN)
                if router:
                    rlink, rdone = chain(dve, dve_router_chain, b - 1, ROUTER_CHAIN)
                for k in range(KC):
                    feature(b, k, f"lin_q{k}", lin_q[:, k, :], link)
                if router:
                    residual(b - 1, rlink)
                feature(b, KC, "lin_kv0", lin_k[:, 0, :], link)
                if router:
                    attended(b - 1, rlink)
                feature(b, KC + 1, "lin_kv1", lin_k[:, 1, :], link)
                if router:
                    tokens(b - 1)
                values(b, 0)
                ps, free = own("lin_sum", b)
                for k in range(KC):
                    last = dve.tensor_tensor(lin_kv[:, k, :], ps[:, k * NL:k * NL + NL], own_head, ALU.mult)
                last.then_inc(free, 1)
                values(b, 1)
                for t in range(TT):
                    ps, free = own(f"lin_out{t}", b)
                    sums = ps[:, 0:KC * NL].rearrange("p (k c) -> p k c", k=KC)
                    link(dve.tensor_scalar(lin_den[:, t, :, :], sums[:, :, P:NL], EPS_LIN, None, ALU.add))
                    link(dve.reciprocal(lin_den[:, t, :, :], lin_den[:, t, :, :]))
                    for k in range(KC):
                        last = dve.tensor_tensor(
                            lin_a[:, t, k * P:k * P + P].rearrange("p (h d) -> p h d", d=LD),
                            ps[:, k * NL:k * NL + P].rearrange("p (h d) -> p h d", d=LD),
                            lin_den[:, t, k, :].unsqueeze(2).to_broadcast([P, HP, LD]), ALU.mult)
                    last.then_inc(free, 1)
                    k, n = gen_at(b, f"lin_out{t}")
                    dve.wait_ge(gen_free[k], n)
                    dve.sem_inc(lin_a_ready, 1)
                values(b, 2)
                if router:
                    router_choice(b - 1, rlink)
                values(b, 3)
                if router:
                    router_slots(b - 1, rlink)
                    assert rdone[0] == ROUTER_CHAIN, rdone
                ps, free = own("lin_proj", b)
                dve.wait_ge(x_bias_ready, b + 1)
                dve.tensor_tensor(z[:, :, :], ps[:, :].rearrange("p (t c) -> p t c", t=TT), x_in[:, :, :],
                                  ALU.add).then_inc(free, 1)
                k, n = gen_at(b, "lin_proj")
                dve.wait_ge(gen_free[k], n)
                moments(z, stats, mv, var_eps, link, var_ready)
                keys(b, 0)
                dve.wait_ge(rstd_ready, 2 * b + 1)
                normalise(x1, z, mv, rstd, x1_ready)
                values(b, 4)
                rest(b, "x1_t", x1_t[0][:, :, :].rearrange("p a b -> p (a b)"),
                     x1_t[1][:, :, :].rearrange("p a b -> p (a b)"), 512)
                keys(b, 1)
                queries(b, 0)
                values(b, 5)
                for s in range(STEPS + 10):
                    j, r = divmod(s - 8, 4)
                    if 0 <= j < PAIRS and r == 0:
                        dve.wait_ge(out_full, STEPS * b + 4 * j + 4)
                        link(dve.reciprocal(inv_total[:, :], total[:, 4 * j:4 * j + 4]))
                        if j >= 2:
                            k, n = gen_at(b, f"o_t{j - 2}")
                            dve.wait_ge(gen_full[k], n)
                        for i in range(2):
                            last = dve.tensor_tensor(
                                o_s[:, j % 2, :, i * DK:i * DK + DK],
                                out_ps[:, i * P:i * P + P].rearrange("p (t d) -> p t d", t=TT),
                                inv_total[:, 2 * i:2 * i + 2].unsqueeze(2).to_broadcast([P, TT, DK]), ALU.mult)
                        last.then_inc(o_ready, 1)
                    j = s // 4
                    if s < STEPS:
                        wait(dve, prob_ready, STEPS * b + s - 1)
                        if s % 4 == 0:
                            dve.wait_ge(mask_ready, PAIRS * b + j + 1)
                        dve.wait_ge(score_full, STEPS * b + s + 1)
                        stand(dve, dve_stood)
                        dve.tensor_tensor_reduce(masked[:, s % 2, :], score[s % 2][:, 0:NKP],
                                                 mask_add[:, s % (4 * RING), :], -SCALE, 3e38, ALU.add, ALU.min,
                                                 low[:, s:s + 1]).then_inc(masked_ready, 1)
                    if s >= 4 and s % 4 == 0 and j + 1 < PAIRS:
                        keys(b, j + 1)
                    if s % 4 == 1 and j + 1 < PAIRS:
                        queries(b, j + 1)
                    j, r = divmod(s - 9, 4)
                    if 0 <= j < PAIRS and r == 0:
                        rest(b, f"o_t{j}", o_t[0][:, j % 2, :], o_t[1][:, j % 2, :], S)
                assert done[0] == CHAIN, done

            for half in q_z:
                last = dve.memset(half[:, :, :].bitcast(F32), 0.0)
            last.then_inc(dve_zeros, 1)
            for half in k_t:
                last = dve.memset(half[:, :, NK:NKP].bitcast(F32), 0.0)
            last.then_inc(dve_zeros, 1)
            dve.memset(seen[:, :, :], 0.0).then_inc(dve_zeros, 1)
            for n, (src, halves) in enumerate(stages):
                dve.wait_ge(stage_rounded, n + 1)
                dve.tensor_tensor(halves[1], v_s[:, n % 3, 0:src.shape[-1]], plain(halves[0]),
                                  ALU.subtract).then_inc(stage_split, 1)
            dve.wait_ge(stage_split, len(stages))
            dve.wait_ge(dve_zeros, 3)
            dve.wait_ge(consts_loaded, 16)
            dve.wait_ge(weights_loaded, len(whole) * 16)
            batch(0)
            with dve.Fori(1, B) as b:
                batch(b)
            rlink, _ = chain(dve, dve_router_chain, B - 1, ROUTER_CHAIN)
            residual(B - 1, rlink)
            attended(B - 1, rlink)
            tokens(B - 1)
            router_choice(B - 1, rlink)
            router_slots(B - 1, rlink)

        @block.gpsimd
        def _(pool):
            def power(dst, src, ready):
                pool.tensor_tensor(dst[:, :], src[:, :], half_pow[:, :], ALU.pow).then_inc(ready, 1)

            def mask(b, j):
                u = j // 2
                if j % 2 == 0:
                    pool.wait_ge(mask_loaded[u % 2], 16 * (2 * b + u // 2 + 1))
                wait(pool, masked_ready, STEPS * b + 4 * (j - RING) + 4)
                stand(pool, pool_stood)
                slot, part = j % RING * 4, j % 2 * 4
                pool.tensor_scalar(mask_add[:, slot:slot + 4, 0:S], mask_in[:, u % 2, part:part + 4, :], MASKED, 1.0,
                                   ALU.mult, ALU.mult).then_inc(mask_ready, 1)

            def split_in(b, src, halves, loaded, half, ready):
                pool.wait_ge(loaded, 16 * b + 16)
                stand(pool, pool_stood)
                pool.tensor_copy(halves[0][:, :, :], src).then_inc(half, 1)
                pool.wait_ge(half, b + 1)
                pool.tensor_tensor(halves[1][:, :, :], src, halves[0][:, :, :].bitcast(F32), ALU.subtract).then_inc(ready, 1)

            def split_x(b):
                if not is_zero(b):
                    k, n = gen_at(b - 1, "lin_kv1")
                    pool.wait_ge(gen_full[k], n)
                split_in(b, x_t_in[:, :, :], x_t, x_t_loaded, x_rounded, x_split)

            def split_f(b):
                split_in(b, f_t_in[:, :, 0:S], f_t, f_t_loaded, f_rounded, f_split)

            def router_root(r):
                pool.wait_ge(r_var_ready, r + 1)
                power(r_rstd, r_var, r_rstd_ready)

            def router_affine(r):
                pool.wait_ge(normed_ready, r + 1)
                for n, op in ((2, ALU.mult), (3, ALU.add)):
                    for t in range(TT):
                        last = pool.tensor_tensor(tok[:, t, :], tok[:, t, :], row_bias[:, n, :], op)
                    if n == 2:
                        last.then_inc(affine_half, 1)
                        pool.wait_ge(affine_half, r + 1)
                last.then_inc(tok_ready, 1)

            def router_scatter(r):
                pool.wait_ge(scatter_ready, r + 1)
                pool.wait_ge(tok_ready, r + 1)
                stand(pool, pool_stood)
                for t in range(TT):
                    pool.indirect_dma_start(
                        out=slots_dram, out_offset=bass.IndirectOffsetOnAxis(ap=scatter_at[:, t:t + 1], axis=0),
                        in_=tok[:, t, :], in_offset=None, bounds_check=last_slot, oob_is_err=False
                    ).then_inc(scattered, 16)

            def batch(b, last_batch=False):
                router = not is_zero(b)
                if router:
                    pool.wait_ge(var_ready, 2 * b)
                    power(rstd, var_eps, rstd_ready)
                    router_root(b - 1)
                pool.wait_ge(x_loaded, 16 * b + 16)
                for t in range(TT):
                    last = pool.tensor_tensor(x_in[:, t, :], x_in[:, t, :], row_bias[:, 0, :], ALU.add)
                last.then_inc(x_bias_ready, 1)
                if router:
                    router_affine(b - 1)
                mask(b, 0)
                mask(b, 1)
                pool.wait_ge(var_ready, 2 * b + 1)
                power(rstd, var_eps, rstd_ready)
                if router:
                    router_scatter(b - 1)
                k, n = gen_at(b, "x1_t")
                pool.wait_ge(gen_full[k], n)
                for t in range(TT):
                    last = pool.tensor_tensor(x1[:, t, :], x1[:, t, :], row_bias[:, 1, :], ALU.add)
                last.then_inc(x1_bias_ready, 1)
                for j in range(2, PAIRS):
                    mask(b, j)
                    if j == 4 and not last_batch:
                        split_x(b + 1)
                if not last_batch:
                    split_f(b + 1)
                if router:
                    pool.wait_ge(scattered, 32 * b)
                pool.sem_inc(scatter_done, 1)

            last_slot = pool.to_reg(E * CAP - 1)
            pool.memset(tok[:, :, :], 0.0).then_inc(pool_zeros, 1)
            pool.memset(half_pow[:, :], -0.5)
            pool.memset(mask_add[:, :, S:NK], 0.0)
            pool.memset(mask_add[:, :, NK:NKP], MASKED)
            pool.memset(prob[:, :, NK:PW], 0.0)
            pool.memset(lin_v[:, :, :, P:NL], 1.0).then_inc(pool_zeros, 1)
            pool.wait_ge(pool_zeros, 2)
            split_x(0)
            split_f(0)
            pool.wait_ge(weights_loaded, len(whole) * 16)
            pool.wait_ge(slots_zeroed, 16 * ZEROED)
            batch(0)
            with pool.Fori(1, B - 1) as b:
                batch(b)
            batch(B - 1, last_batch=True)
            pool.wait_ge(var_ready, 2 * B)
            power(rstd, var_eps, rstd_ready)
            router_root(B - 1)
            router_affine(B - 1)
            router_scatter(B - 1)
            pool.wait_ge(scattered, 32 * B)


def is_zero(b):
    return isinstance(b, int) and b == 0


def batch_of(ap, b, rows=slice(None)):
    return ap[bass.ds(b, 1), :, rows, :].rearrange("b p r c -> p (b r) c")


def experts(nc, io, consts, slots_dram, rows_dram):
    with ExitStack() as ctx:
        def sb(name, shape, dt=F32):
            return ctx.enter_context(nc.sbuf_tensor(name, shape, dt))

        def sem(name):
            return ctx.enter_context(nc.semaphore(name))

        ident = consts[:, 0:P]
        wi = [sb(f"wi{i}", [P, KC, I]) for i in range(2)]
        wo = [sb(f"wo_e{i}", [P, IT, C]) for i in range(2)]
        slots = [sb(f"slots{i}", [P, ST, C]) for i in range(2)]
        slots_t = sb("slots_t", [P, KC, CAP])
        hidden = sb("hidden", [P, IT, CAP])
        rows = sb("rows", [P, ST, C])
        ps_t = [ctx.enter_context(nc.psum_tensor(f"ps_t{i}", [P, 512], F32)) for i in range(2)]
        ps_h = [ctx.enter_context(nc.psum_tensor(f"ps_h{i}", [P, 512], F32)) for i in range(2)]
        ps_o = [ctx.enter_context(nc.psum_tensor(f"ps_o{i}", [P, 512], F32)) for i in range(2)]
        loaded = [sem("loaded0"), sem("loaded1")]
        t_full, t_ready = sem("t_full"), sem("t_ready")
        h_full, h_ready = sem("h_full"), sem("h_ready")
        o_full, o_ready = sem("o_full_e"), sem("o_ready_e")
        rows_stored, e_stood = sem("rows_stored"), sem("e_stood")
        PER = 3 * 16
        slot_tiles = slots_dram.rearrange("(e t p) c -> e p t c", t=ST, p=P)
        row_tiles = rows_dram.rearrange("(e t p) c -> e p t c", t=ST, p=P)

        block = ctx.enter_context(nc.Block())

        @block.sync
        def _(sp):
            def load(g, i):
                sp.dma_start(slots[i][:, :, :], batch_of(slot_tiles, 2 * g + i)).then_inc(loaded[i], 16)
                sp.dma_start(wi[i][:, :, :], batch_of(io["wi"], 2 * g + i)).then_inc(loaded[i], 16)
                sp.dma_start(wo[i][:, :, :], batch_of(io["wo_e"], 2 * g + i)).then_inc(loaded[i], 16)

            def store(g, i):
                e = 2 * g + i
                sp.wait_ge(o_ready, 2 * e + 2)
                stand(sp, e_stood)
                sp.dma_start(batch_of(row_tiles, e), rows[:, :, :]).then_inc(rows_stored, 16)

            load(0, 0)
            load(0, 1)
            with sp.Fori(1, E // 2) as g:
                for i in range(2):
                    store(g - 1, i)
                    load(g, i)
            store(E // 2 - 1, 0)
            store(E // 2 - 1, 1)
            sp.wait_ge(rows_stored, 16 * E)

        def pairs_of_experts(eng, expert):
            for i in range(2):
                expert(0, i, i)
            with eng.Fori(1, E // 2) as g:
                for i in range(2):
                    expert(g, i, 2 * g + i)

        @block.tensor
        def _(pe):
            def expert(g, i, e):
                pe.wait_ge(loaded[i], PER * g + PER)
                for k in range(KC):
                    for t in range(ST):
                        mm = pe.transpose(ps_t[k][:, t * P:t * P + P], slots[i][:, t, k * P:k * P + P], ident)
                    mm.then_inc(t_full, 1)
                pe.wait_ge(t_ready, KC * e + KC)
                for f in range(IT):
                    wait(pe, h_ready, IT * e + f - 1)
                    for k in range(KC):
                        mm = pe.matmul(ps_h[f % 2][:, :], wi[i][:, k, f * P:f * P + P], slots_t[:, k, :],
                                       start=(k == 0), stop=(k == KC - 1))
                    mm.then_inc(h_full, 1)
                pe.wait_ge(h_ready, IT * e + IT)
                for v in range(ST // 2):
                    wait(pe, o_ready, 2 * e + v - 1)
                    for u in (2 * v, 2 * v + 1):
                        for f in range(IT):
                            mm = pe.matmul(ps_o[v][:, (u % 2) * C:(u % 2) * C + C], hidden[:, f, u * P:u * P + P],
                                           wo[i][:, f, :], start=(f == 0), stop=(f == IT - 1))
                    mm.then_inc(o_full, 1)
            pairs_of_experts(pe, expert)

        @block.scalar
        def _(act):
            def expert(g, i, e):
                for f in range(IT):
                    act.wait_ge(h_full, IT * e + f + 1)
                    act.activation(hidden[:, f, :], ps_h[f % 2][:, :], ACT.Gelu).then_inc(h_ready, 1)
            pairs_of_experts(act, expert)

        @block.vector
        def _(dve):
            def expert(g, i, e):
                for k in range(KC):
                    dve.wait_ge(t_full, KC * e + k + 1)
                    dve.tensor_copy(slots_t[:, k, :], ps_t[k][:, :]).then_inc(t_ready, 1)
                for v in range(ST // 2):
                    dve.wait_ge(o_full, 2 * e + v + 1)
                    wait(dve, rows_stored, 16 * e)
                    dve.tensor_copy(rows[:, 2 * v:2 * v + 2, :],
                                    ps_o[v][:, :].rearrange("p (t c) -> p t c", t=2)).then_inc(o_ready, 1)
            pairs_of_experts(dve, expert)


def combine(nc, io, weight, gather_at, half_pow, x2_dram, rows_dram):
    R = 4
    with ExitStack() as ctx:
        def sb(name, shape, dt=F32):
            return ctx.enter_context(nc.sbuf_tensor(name, shape, dt))

        def sem(name):
            return ctx.enter_context(nc.semaphore(name))

        at = sb("at", [P, R, TT], I32)
        w = sb("w", [P, R, TT])
        got = sb("got", [P, R, TT, C])
        base = sb("base", [P, R, TT, C])
        y = sb("y", [P, R, TT, C])
        res = sb("res", [P, R, TT, C])
        st = sb("st", [P, R, TT, 6])
        m = sb("m", [P, R, TT, 2])
        var = sb("var", [P, R, TT])
        root = sb("root", [P, R, TT])
        at_ready, w_ready = sem("at_ready"), sem("w_ready")
        gathered = [sem(f"gathered{i}") for i in range(R)]
        base_in = [sem(f"base_in{i}") for i in range(R)]
        stored = [sem(f"stored{i}") for i in range(R)]
        y_ready, var_done, root_done, res_ready = sem("y_ready"), sem("var_done"), sem("root_done"), sem("res_ready")
        steps, stood, c_sp_stood, c_pool_stood = (
            sem("c_steps"), sem("c_stood"), sem("c_sp_stood"), sem("c_pool_stood"))
        STEPS_C = 2

        block = ctx.enter_context(nc.Block())

        def rings(eng, batch):
            for i in range(R):
                batch(0, i, i)
            with eng.Fori(1, B // R) as g:
                for i in range(R):
                    batch(g, i, g * R + i)

        @block.sync
        def _(sp):
            def load(g, i, b):
                wait(sp, y_ready, b - R + 1)
                stand(sp, c_sp_stood)
                sp.dma_start(base[:, i, :, :], batch_of(x2_dram, b)).then_inc(base_in[i], 16)

            def store(g, i, b):
                sp.wait_ge(res_ready, b + 1)
                stand(sp, c_sp_stood)
                sp.dma_start(batch_of(io["out"], b), res[:, i, :, :]).then_inc(stored[i], 16)

            for i in range(R):
                load(0, i, i)
            with sp.Fori(1, B // R) as g:
                for i in range(R):
                    load(g, i, g * R + i)
                    store(g - 1, i, g * R + i - R)
            for i in range(R):
                store(B // R - 1, i, B - R + i)
            for i in range(R):
                sp.wait_ge(stored[i], 16 * (B // R))

        @block.gpsimd
        def _(pool):
            last_slot = pool.to_reg(E * CAP - 1)

            def gather(g, i, b):
                pool.wait_ge(at_ready, b + 1)
                wait(pool, y_ready, b - R + 1)
                stand(pool, c_pool_stood)
                for t in range(TT):
                    pool.indirect_dma_start(
                        out=got[:, i, t, :], out_offset=None, in_=rows_dram,
                        in_offset=bass.IndirectOffsetOnAxis(ap=at[:, i, t:t + 1], axis=0),
                        bounds_check=last_slot, oob_is_err=False).then_inc(gathered[i], 16)

            def power(i, b):
                pool.wait_ge(var_done, b + 1)
                pool.tensor_tensor(root[:, i, :], var[:, i, :], half_pow[:, :], ALU.pow).then_inc(root_done, 1)

            gather(0, 0, 0)
            gather(0, 1, 1)
            for i in range(2, R):
                gather(0, i, i)
                power(i - 2, i - 2)
            with pool.Fori(1, B // R) as g:
                for i in range(R):
                    gather(g, i, g * R + i)
                    power((i - 2) % R, g * R + i - 2)
            for b in (B - 2, B - 1):
                power(b % R, b)

        @block.vector
        def _(dve):
            def pick(g, i, b):
                if not is_zero(g):
                    dve.wait_ge(gathered[i], 32 * g)
                dve.tensor_copy(at[:, i, :], gather_at[:, bass.ds(b * TT, TT)]).then_inc(at_ready, 1)

            def front(g, i, b):
                dve.tensor_scalar(w[:, i, :], weight[:, bass.ds(b * TT, TT)], 0.5, None, ALU.mult).then_inc(w_ready, 1)
                dve.wait_ge(w_ready, b + 1)
                dve.wait_ge(gathered[i], 32 * g + 32)
                dve.wait_ge(base_in[i], 16 * g + 16)
                for t in range(TT):
                    last = dve.scalar_tensor_tensor(out=y[:, i, t, :], in0=got[:, i, t, :], scalar=w[:, i, t:t + 1],
                                                    in1=base[:, i, t, :], op0=ALU.mult, op1=ALU.add)
                last.then_inc(y_ready, 1)
                dve.wait_ge(y_ready, b + 1)
                for t in range(TT):
                    last = dve.bn_stats(st[:, i, t, :], y[:, i, t, :])
                last.then_inc(steps, 1)
                dve.wait_ge(steps, STEPS_C * b + 1)
                stand(dve, stood)
                for t in range(TT):
                    last = dve.bn_aggr(m[:, i, t, :], st[:, i, t, :])
                last.then_inc(steps, 1)
                dve.wait_ge(steps, STEPS_C * b + 2)
                dve.tensor_scalar(var[:, i, :], m[:, i, :, 1], EPS_LN / 4, None, ALU.add).then_inc(var_done, 1)

            def back(g, i, b):
                dve.wait_ge(root_done, b + 1)
                wait(dve, stored[i], 16 * g)
                for t in range(TT):
                    last = dve.tensor_scalar(res[:, i, t, :], y[:, i, t, :], m[:, i, t, 0:1], root[:, i, t:t + 1],
                                             ALU.subtract, ALU.mult)
                last.then_inc(res_ready, 1)

            for i in range(R):
                pick(0, i, i)
            for i in range(R):
                front(0, i, i)
                if i >= 2:
                    back(0, i - 2, i - 2)

            def ring(g):
                for i in range(R):
                    pick(g, i, g * R + i)
                for i in range(R):
                    front(g, i, g * R + i)
                    back(g if i >= 2 else g - 1, (i - 2) % R, g * R + i - 2)

            ring(1)
            with dve.Fori(2, B // R) as g:
                ring(g)
            for i in (R - 2, R - 1):
                back(B // R - 1, i, B - R + i)


def _layout(a):
    import numpy as np

    f = {k: np.asarray(v) for k, v in a.items()}

    def channels_first(w):
        return w.T.reshape(-1, P, w.shape[0]).transpose(1, 0, 2)

    def batch_channels_first(v):
        return v.transpose(0, 2, 1).reshape(v.shape[0], KC, P, v.shape[1]).transpose(0, 2, 1, 3)

    def on_all_partitions(*rows):
        return np.broadcast_to(np.stack(rows)[None], (P, len(rows), rows[0].shape[0]))

    head = np.arange(P) // LD
    consts = np.concatenate([
        np.eye(P), np.triu(np.ones((P, P)), 1), np.ones((P, P)),
        head[:, None] == head[None], head[:, None] == np.arange(HP)[None],
        np.broadcast_to(np.arange(E)[None], (P, E))], axis=1).astype(np.float32)
    x = f["x"]
    mask = f["mask_Bx16xSxS_bk1"]
    out = {
        "consts": consts,
        "x": x.reshape(B, TT, P, C).transpose(0, 2, 1, 3),
        "x_t": batch_channels_first(x),
        "f_t": np.concatenate([batch_channels_first(f["fside_BxSxS_0"]), batch_channels_first(f["ctx_1024"])], axis=3),
        "mask": mask.reshape(B, XH, TT, P, S).transpose(0, 3, 1, 2, 4).reshape(B, P, STEPS, S),
        "wqkv": channels_first(f["L0_attn_Wqkv"]),
        "wproj": channels_first(f["L0_attn_Wproj"]),
        "wq": channels_first(f["L0_xattn_Wq"]),
        "wk": channels_first(f["L0_xattn_Wk"]),
        "wgk": channels_first(f["L0_xattn_Wgk"]),
        "wv": channels_first(f["L0_xattn_Wv"]),
        "wgv": channels_first(f["L0_xattn_Wgv"]),
        "wo": channels_first(f["L0_xattn_Wo"]),
        "wgate": channels_first(f["L0_ffn_gate_weight"]),
        "col_bias": np.stack([f["L0_xattn_bq"], f["L0_xattn_bk"], f["L0_xattn_bgk"]]).reshape(3, PAIRS, P).transpose(2, 0, 1),
        "row_bias": on_all_partitions(f["L0_attn_bproj"], f["L0_xattn_bo"], f["L0_ffn_ln_gamma"], f["L0_ffn_ln_beta"]),
        "v_bias": on_all_partitions(f["L0_xattn_bv"], f["L0_xattn_bgv"]),
        "wi": f["L0_ffn_wi"].reshape(E, KC, P, I).transpose(0, 2, 1, 3),
        "wo_e": f["L0_ffn_wo"].reshape(E, IT, P, C).transpose(0, 2, 1, 3),
    }
    return {k: np.ascontiguousarray(v) for k, v in out.items()}


def kernel(**inputs):
    import numpy as np
    import concourse.bacc as bacc
    from concourse.bass_utils import run_bass_kernel_spmd

    arrays = _layout(inputs)
    nc = bacc.Bacc("TRN2", target_bir_lowering=False, num_devices=1)
    io = {name: nc.dram_tensor("in_" + name, a.shape, mybir.dt.from_np(a.dtype), kind="ExternalInput").ap()
          for name, a in arrays.items()}
    io["out"] = nc.dram_tensor("out", (B, P, TT, C), F32, kind="ExternalOutput").ap()
    decoder_kernel(nc, io)
    r = run_bass_kernel_spmd(nc, [{"in_" + name: a for name, a in arrays.items()}], core_ids=[0])
    out = r.results[0]["out"]
    return np.ascontiguousarray(out.transpose(0, 2, 1, 3)).reshape(B, S, C)
```

```python
from contextlib import ExitStack

import concourse.bass as bass
from concourse import mybir

ALU = mybir.AluOpType
ACT = mybir.ActivationFunctionType
AX = mybir.AxisListType
F32 = mybir.dt.float32
BF16 = mybir.dt.bfloat16
U8 = mybir.dt.uint8
F32R = mybir.dt.float32r
I32 = mybir.dt.int32
U32 = mybir.dt.uint32

P = 128
B, S, C = 32, 256, 256
TT = S // P
KC = C // P
LD = 16
HP = P // LD
XH, DK = 16, 64
XF = XH * DK
PAIRS = XH // 2
G = 77
NK = S + G
KT_TILES = (P, P, G)
PW = 3 * P
STEPS = XH * TT
E, I = 8, 1024
CAP = 512
ST = CAP // P
IT = I // P
TILES = B * TT
EPS_LIN = 1e-6
EPS_LN = 1e-5
MASKED = -1e30
SCALE = DK ** -0.5
NL = LD * HP + HP

NKP = NK + 1
RING = 2

ROUTER = ["tok_t0", "tok_t1", "logits", "rank"]
OWN = ["lin_q0", "lin_q1", "lin_kv0", "lin_kv1", "lin_sum", "lin_out0", "lin_out1", "tok_t0", "tok_t1", "lin_t",
       "logits", "lin_proj", "rank", "x1_t", "q0"]
for _s in range(1, 4 * PAIRS + 8):
    if _s % 4 == 1 and _s // 4 + 1 < PAIRS:
        OWN.append(f"q{_s // 4 + 1}")
    if _s % 4 == 3 and 0 <= (_s - 11) // 4 < PAIRS:
        OWN.append(f"o_t{(_s - 11) // 4}")
    if _s % 4 == 3 and _s // 4 + 2 < PAIRS:
        OWN.append(f"k{_s // 4 + 2}")
FILLS = [n for n in OWN if n not in ROUTER], OWN, ROUTER
assert all(len(f) % 2 == 0 for f in FILLS)

CHAIN = 10 + PAIRS
ROUTER_CHAIN = 17
ROUNDED = ["k0", "k1"]
for _n in OWN:
    if _n[0] == "q":
        ROUNDED.append(_n + "_even")
    if _n == "x1_t" or _n[0] in "kq" or _n[:3] == "o_t":
        ROUNDED.append(_n)


def wait(eng, sem, value):
    if not isinstance(value, int) or value > 0:
        eng.wait_ge(sem, value)


def stand(eng, sem):
    eng.sem_inc(sem, 1)


def gen_at(b, name):
    if name[0] == "v":
        n = int(name[1:])
        return 2 + n % 2, 3 * b + n // 2 + 1
    if name in ("k0", "k1"):
        return 4 + int(name[1:]), b + 1
    first, other, last = FILLS
    if is_zero(b):
        before, fills = 0, first
    else:
        before = (len(first) - len(other)) // 2 + b * (len(other) // 2)
        fills = last if isinstance(b, int) and b == B else other
    n = fills.index(name)
    return n % 2, before + n // 2 + 1


def rounded_at(b, name):
    return b * len(ROUNDED) + ROUNDED.index(name) + 1


def chain(eng, sem, b, per_batch):
    done = [0]

    def link(ins):
        done[0] += 1
        assert done[0] <= per_batch
        ins.then_inc(sem, 1)
        eng.wait_ge(sem, b * per_batch + done[0])
    return link, done


def decoder_kernel(nc, io):
    with ExitStack() as keep:
        def dram(name, shape):
            return nc.dram_tensor(name, shape, F32, kind="Internal").ap()

        x2_dram = dram("x2_dram", [B, P, TT, C])
        slots_dram = dram("slots_dram", [E * CAP, C])
        rows_dram = dram("rows_dram", [E * CAP, C])

        consts = keep.enter_context(nc.sbuf_tensor("consts", [P, 3 * P + NL + E], F32))
        weight = keep.enter_context(nc.sbuf_tensor("weight", [P, TILES], F32))
        gather_at = keep.enter_context(nc.sbuf_tensor("gather_at", [P, TILES], I32))
        half_pow = keep.enter_context(nc.sbuf_tensor("half_pow", [P, TT], F32))
        attention_and_router(nc, io, consts, weight, gather_at, half_pow, x2_dram, slots_dram)
        experts(nc, io, consts, slots_dram, rows_dram)
        combine(nc, io, weight, gather_at, half_pow, x2_dram, rows_dram)


def attention_and_router(nc, io, consts, weight, gather_at, half_pow, x2_dram, slots_dram):
    with ExitStack() as ctx:
        def sb(name, shape, dt=F32):
            return ctx.enter_context(nc.sbuf_tensor(name, shape, dt))

        def split(name, shape):
            return sb(name + "_hi", shape, F32R), sb(name + "_lo", shape, F32R)

        def sem(name):
            return ctx.enter_context(nc.semaphore(name))

        def bank(name):
            return ctx.enter_context(nc.psum_tensor(name, [P, 512], F32))

        ident = consts[:, 0:P]
        before = consts[:, P:2 * P]
        ones = consts[:, 2 * P:3 * P]
        own_head = consts[:, 3 * P:3 * P + NL]
        expert_no = consts[:, 3 * P + NL:3 * P + NL + E]

        wqkv = split("wqkv", [P, KC, 3 * C])
        wproj = sb("wproj", [P, KC, C])
        wq = split("wq", [P, KC, XF])
        wk = split("wk", [P, KC, XF])
        wgk = sb("wgk", [P, KC, XF])
        wv = split("wv", [P, KC, XF])
        wgv = sb("wgv", [P, KC, XF])
        wo = split("wo", [P, PAIRS, C])
        wgate = sb("wgate", [P, KC, E])
        col_bias = sb("col_bias", [P, 3, PAIRS])
        row_bias = sb("row_bias", [P, 4, C])
        v_bias = sb("v_bias", [P, 2, XF])
        x_t_in = sb("x_t_in", [P, KC, S])
        x_t = split("x_t", [P, KC, S])
        x_in = sb("x_in", [P, TT, C])
        f_t_in = sb("f_t_in", [P, KC, NK])
        f_t = split("f_t", [P, KC, S])
        mask_in = sb("mask_in", [P, 2, STEPS // 4, S], U8)
        mask_add = sb("mask_add", [P, 4 * RING, NKP], BF16)
        e_x = sb("e_x", [P, 4, C])
        lin_q = sb("lin_q", [P, KC, S])
        lin_k = sb("lin_k", [P, TT, C])
        lin_v = sb("lin_v", [P, TT, KC, NL])
        lin_kv = sb("lin_kv", [P, KC, NL])
        lin_den = sb("lin_den", [P, TT, KC, HP])
        lin_at = sb("lin_at", [P, KC, S])
        z = sb("z", [P, TT, C])
        lin_a = z
        stats = sb("stats", [P, TT, 6])
        mv = sb("mv", [P, TT, 2])
        var_eps = sb("var_eps", [P, TT])
        rstd = sb("rstd", [P, TT])
        x1 = sb("x1", [P, TT, C])
        x1_t = split("x1_t", [P, KC, S])
        q_d = sb("q_d", [P, 2 * RING, S], F32R)
        k_d = sb("k_d", [P, 2 * RING, 2, NKP], F32R)
        v_s = sb("v_s", [P, 3, XF])
        masked = sb("masked", [P, 2, NKP])
        low = sb("low", [P, STEPS])
        prob = sb("prob", [P, 4, PW])
        total = sb("total", [P, STEPS])
        inv_total = sb("inv_total", [P, 4])
        prob_t = sb("prob_t", [P, 2, PW])
        o_s = sb("o_s", [P, 2, TT, P])
        o_t = split("o_t", [P, 2, S])
        x2 = sb("x2", [P, TT, C])
        tok = sb("tok", [P, TT, C])
        tok_t = sb("tok_t", [P, KC, S])
        r_stats = sb("r_stats", [P, TT, 6])
        r_mv = sb("r_mv", [P, TT, 2])
        r_var = sb("r_var", [P, TT])
        r_rstd = sb("r_rstd", [P, TT])
        logit = sb("logit", [P, TT, E])
        top = sb("top", [P, TT, 8])
        top_at = sb("top_at", [P, TT, 8], U32)
        top_f = sb("top_f", [P, TT])
        rel = sb("rel", [P, TT, E])
        e_rel = sb("e_rel", [P, TT, E])
        e_sum = sb("e_sum", [P, TT])
        p_top = sb("p_top", [P, TT])
        onehot = sb("onehot", [P, TT, E])
        seen = sb("seen", [P, TT, E])
        own_rank = sb("own_rank", [P, TT, E])
        rank = sb("rank", [P, TT])
        kept_rank = sb("kept_rank", [P, TT])
        beyond = sb("beyond", [P, TT])
        slot_f = sb("slot_f", [P, TT])
        scatter_at = sb("scatter_at", [P, TT], I32)

        score = [bank("score0"), bank("score1")]
        prt = [bank("prt0"), bank("prt1")]
        gen = [bank("gen0"), bank("gen1")] + prt + score
        out_ps = bank("out_ps")
        o_proj = bank("o_proj")

        consts_loaded, weights_loaded = sem("consts_loaded"), sem("weights_loaded")
        x_t_loaded, x_loaded, f_t_loaded = sem("x_t_loaded"), sem("x_loaded"), sem("f_t_loaded")
        mask_loaded = [sem(f"mask_loaded{i}") for i in range(2)]
        staged = [sem(f"staged{i}") for i in range(3)]
        stage_rounded, stage_split = sem("stage_rounded"), sem("stage_split")
        x_split, f_split, f_rounded = sem("x_split"), sem("f_split"), sem("f_rounded")
        x_rounded = sem("x_rounded")
        slots_zeroed, scattered, scatter_done = sem("slots_zeroed"), sem("scattered"), sem("scatter_done")
        x2_stored, x2_free = sem("x2_stored"), sem("x2_free")
        pool_zeros, dve_zeros = sem("pool_zeros"), sem("dve_zeros")
        gen_full = [sem(f"gen_full{i}") for i in range(6)]
        gen_free = [sem(f"gen_free{i}") for i in range(6)]
        o_proj_full, o_proj_free = sem("o_proj_full"), sem("o_proj_free")
        rounded = sem("rounded")
        score_full, prt_full, out_full = sem("score_full"), sem("prt_full"), sem("out_full")
        exp_ready, lin_a_ready = sem("exp_ready"), sem("lin_a_ready")
        x_bias_ready, x1_bias_ready = sem("x_bias_ready"), sem("x1_bias_ready")
        var_ready, rstd_ready = sem("var_ready"), sem("rstd_ready")
        x1_ready, x2_ready = sem("x1_ready"), sem("x2_ready")
        mask_ready, masked_ready = sem("mask_ready"), sem("masked_ready")
        values_ready = sem("values_ready")
        keys_copied = [sem(f"keys_copied{i}") for i in range(2)]
        prob_ready, prob_t_ready, o_ready = sem("prob_ready"), sem("prob_t_ready"), sem("o_ready")
        normed_ready, tok_ready = sem("normed_ready"), sem("tok_ready")
        r_var_ready, r_rstd_ready = sem("r_var_ready"), sem("r_rstd_ready")
        rel_ready, e_rel_ready = sem("rel_ready"), sem("e_rel_ready")
        seen_ready, scatter_ready = sem("seen_ready"), sem("scatter_ready")
        dve_chain, dve_router_chain = sem("dve_chain"), sem("dve_router_chain")
        affine_half = sem("affine_half")
        dve_stood, pool_stood, sp_stood = sem("dve_stood"), sem("pool_stood"), sem("sp_stood")

        block = ctx.enter_context(nc.Block())

        stages = []
        for w, name in ((wqkv, "wqkv"), (wv, "wv"), (wk, "wk"), (wq, "wq")):
            stages += [(io[name][:, k, :], [h[:, k, :] for h in w]) for k in range(KC)]
        stages += [(io["wo"][:, k * 4:k * 4 + 4, :].rearrange("p j c -> p (j c)"),
                    [h[:, k * 4:k * 4 + 4, :].rearrange("p j c -> p (j c)") for h in wo]) for k in range(KC)]
        whole = ((wproj, "wproj"), (wgk, "wgk"), (wgv, "wgv"), (wgate, "wgate"), (col_bias, "col_bias"),
                 (row_bias, "row_bias"), (v_bias, "v_bias"))
        ZEROED = E * CAP // (P * TT)

        @block.sync
        def _(sp):
            def copy_keys(b, j):
                k, n = gen_at(b, f"k{j}")
                sp.wait_ge(gen_free[k], n)
                stand(sp, sp_stood)
                for i in range(2):
                    slot = 2 * (j % RING) + i
                    sp.dma_start(k_d[half(1 - i), slot, :, :].bitcast(F32), k_d[half(i), slot, :, :].bitcast(F32)
                                 ).then_inc(keys_copied[j % 2], 16)

            def load_x_t(b):
                wait(sp, x_split, b)
                stand(sp, sp_stood)
                sp.dma_start(x_t_in[:, :, :], batch_of(io["x_t"], b)).then_inc(x_t_loaded, 16)

            def load_x(b):
                if not is_zero(b):
                    k, n = gen_at(b - 1, "lin_proj")
                    sp.wait_ge(gen_free[k], n)
                stand(sp, sp_stood)
                sp.dma_start(x_in[:, :, :], batch_of(io["x"], b)).then_inc(x_loaded, 16)

            def load_f_t(b):
                if not is_zero(b):
                    k, n = gen_at(b - 1, f"k{PAIRS - 1}")
                    sp.wait_ge(gen_free[k], n)
                stand(sp, sp_stood)
                sp.dma_start(f_t_in[:, :, :], batch_of(io["f_t"], b)).then_inc(f_t_loaded, 16)

            def load_mask(b, u):
                wait(sp, mask_ready, PAIRS * b + 2 * u - 2)
                stand(sp, sp_stood)
                n = STEPS // 4
                sp.dma_start(mask_in[:, u % 2, :, :], batch_of(io["mask"], b, slice(u * n, u * n + n))
                             ).then_inc(mask_loaded[u % 2], 16)

            def store(b):
                sp.wait_ge(x2_ready, b + 1)
                stand(sp, sp_stood)
                sp.dma_start(batch_of(x2_dram, b), x2[:, :, :]).then_inc(x2_stored, 16)

            def batch(b, last=False):
                if not last:
                    load_x_t(b + 1)
                if not is_zero(b):
                    store(b - 1)
                if not last:
                    load_x(b + 1)
                copy_keys(b, 0)
                load_mask(b, 2)
                copy_keys(b, 1)
                if not is_zero(b):
                    sp.wait_ge(x2_stored, 16 * b)
                sp.sem_inc(x2_free, 1)
                copy_keys(b, 2)
                copy_keys(b, 3)
                load_mask(b, 3)
                copy_keys(b, 4)
                copy_keys(b, 5)
                if not last:
                    load_mask(b + 1, 0)
                copy_keys(b, 6)
                copy_keys(b, 7)
                if not last:
                    load_mask(b + 1, 1)
                    load_f_t(b + 1)

            load_x_t(0)
            load_f_t(0)
            sp.dma_start(consts[:, :], io["consts"]).then_inc(consts_loaded, 16)
            for n, (src, halves) in enumerate(stages):
                wait(sp, stage_split, n - 2)
                sp.dma_start(v_s[:, n % 3, 0:src.shape[-1]], src).then_inc(staged[n % 3], 16)
            for dst, name in whole:
                sp.dma_start(dst[:, :, :], io[name]).then_inc(weights_loaded, 16)
            load_x(0)
            load_mask(0, 0)
            load_mask(0, 1)
            sp.wait_ge(pool_zeros, 1)
            slot_rows = slots_dram.rearrange("(n p t) c -> n p (t c)", p=P, t=TT)
            for n in range(ZEROED):
                sp.dma_start(slot_rows[n], tok[:, :, :].rearrange("p t c -> p (t c)")).then_inc(slots_zeroed, 16)
            batch(0)
            with sp.Fori(1, B - 1) as b:
                batch(b)
            batch(B - 1, last=True)
            store(B - 1)
            sp.wait_ge(slots_zeroed, 16 * ZEROED)
            sp.wait_ge(x2_stored, 16 * B)

        @block.tensor
        def _(pe):
            def multiply(out, lhs, rhs, tiles, first=True, last=True, **how):
                if isinstance(lhs, tuple):
                    terms = [(lhs[0], rhs[0]), (lhs[0], rhs[1]), (lhs[1], rhs[0])]
                else:
                    terms = [(lhs, rhs)]
                n = len(terms) * tiles
                for k in range(tiles):
                    for i, (x, y) in enumerate(terms):
                        at = k * len(terms) + i
                        mm = pe.matmul(out, x[:, k], y[:, k], start=first and at == 0, stop=last and at == n - 1, **how)
                return mm

            def part(x, *index):
                if isinstance(x, tuple):
                    return tuple(h[(slice(None), slice(None)) + index] for h in x)
                return x[(slice(None), slice(None)) + index]

            def fill(b, name):
                k, n = gen_at(b, name)
                wait(pe, gen_free[k], n - 1)
                return gen[k], gen_full[k]

            def read(b, name):
                k, n = gen_at(b, name)
                pe.wait_ge(gen_free[k], n)

            def project(b, name, parts):
                ps, full = fill(b, name)
                for (c0, c1), lhs, rhs in parts:
                    m = (lhs[0] if isinstance(lhs, tuple) else lhs).shape[-1]
                    mm = multiply(ps[0:m, c0:c1], lhs, rhs, KC)
                mm.then_inc(full, 1)

            def keys(b, j):
                f = slice(j * P, j * P + P)
                project(b, f"k{j}", [((0, S), part(wk, f), f_t), ((S, NK), wgk[:, :, f], f_t_in[:, :, S:NK])])

            def queries(b, j):
                project(b, f"q{j}", [((0, S), part(wq, slice(j * P, j * P + P)), x1_t)])

            def values(b, n):
                t, half = n // 2, n % 2
                f = slice(half * 512, half * 512 + 512)
                if t < 2:
                    project(b, f"v{n}", [((0, 512), part(f_t, slice(t * P, t * P + P)), part(wv, f))])
                else:
                    project(b, f"v{n}", [((0, 512), f_t_in[:, :, S:NK], wgv[:, :, f])])

            def transposes(b, src, name, tiles=range(KC)):
                ps, full = fill(b, name)
                blocks = [(k, t) for k in tiles for t in range(TT)]
                for n, (k, t) in enumerate(blocks):
                    mm = pe.transpose(ps[:, n * P:n * P + P], src[:, t, k * P:k * P + P], ident)
                mm.then_inc(full, 1)

            def router_tokens(r):
                pe.wait_ge(tok_ready, r + 1)
                for k in range(KC):
                    transposes(r + 1, tok, f"tok_t{k}", [k])

            def router_logits(r):
                ps, full = fill(r + 1, "logits")
                for k in range(KC):
                    read(r + 1, f"tok_t{k}")
                for t in range(TT):
                    mm = multiply(ps[:, t * E:t * E + E], tok_t[:, :, t * P:t * P + P], wgate, KC)
                mm.then_inc(full, 1)

            def router_rank(r):
                ps, full = fill(r + 1, "rank")
                pe.wait_ge(seen_ready, r + 1)
                pe.matmul(ps[:, 0:TT * E], before, onehot[:, :, :], start=True, stop=False)
                pe.matmul(ps[:, 0:TT * E], ones, seen[:, :, :], start=False, stop=True).then_inc(full, 1)

            def output(b, j):
                if j == 0:
                    wait(pe, o_proj_free, b)
                read(b, f"o_t{j}")
                for t in range(TT):
                    mm = multiply(o_proj[:, t * C:t * C + C],
                                  tuple(o[:, j % 2:j % 2 + 1, t * P:t * P + P] for o in o_t),
                                  tuple(w[:, j:j + 1, :] for w in wo), 1, first=(j == 0 and t == 0),
                                  last=(j == PAIRS - 1), skip_group_check=True)
                if j == PAIRS - 1:
                    mm.then_inc(o_proj_full, 1)

            def attend(b):
                for s in range(STEPS + 11):
                    j = s // 4
                    if s < STEPS:
                        h, t = s // TT, s % TT
                        if s % 4 == 0:
                            pe.wait_ge(keys_copied[j % 2], 32 * (PAIRS // 2 * b + j // 2 + 1))
                            read(b, f"q{j}")
                        if s == 1:
                            read(b, "k1")
                        wait(pe, masked_ready, STEPS * b + s - 1)
                        slot = h % (2 * RING)
                        for n in range(2):
                            mm = pe.matmul(score[s % 2][:, 0:NKP], q_d[:, slot, t * P:t * P + P],
                                           k_d[:, slot, n, :], start=(n == 0), stop=(n == 1))
                        mm.then_inc(score_full, 1)
                    if s % 4 == 1 and j + 1 < PAIRS:
                        queries(b, j + 1)
                    n = s - 3
                    if 0 <= n < STEPS:
                        if n < 2:
                            read(b, f"v{4 + n}")
                        wait(pe, prob_t_ready, STEPS * b + n - 1)
                        pe.wait_ge(prob_ready, STEPS * b + n + 1)
                        for k in range(3):
                            mm = pe.transpose(prt[n % 2][:, k * P:k * P + P], prob[:, n % 4, k * P:k * P + P], ident)
                        mm.then_inc(prt_full, 1)
                    n = s - 5
                    if 0 <= n < STEPS:
                        h, c = n // TT, n % 4
                        if n == 0:
                            pe.wait_ge(values_ready, 6 * b + 6)
                        if c == 0:
                            wait(pe, o_ready, PAIRS * b + n // 4)
                        pe.wait_ge(prob_t_ready, STEPS * b + n + 1)
                        for k in range(3):
                            rows = KT_TILES[k]
                            mm = pe.matmul(out_ps[:, c * DK:c * DK + DK], prob_t[0:rows, n % 2, k * P:k * P + P],
                                           v_s[0:rows, k, h * DK:h * DK + DK], start=(k == 0), stop=(k == 2))
                        mm.then_inc(out_full, 1)
                    j, r = divmod(s - 11, 4)
                    if 0 <= j < PAIRS and r == 0:
                        ps, full = fill(b, f"o_t{j}")
                        pe.wait_ge(o_ready, PAIRS * b + j + 1)
                        for t in range(TT):
                            mm = pe.transpose(ps[:, t * P:t * P + P], o_s[:, j % 2, t, :], ident)
                        mm.then_inc(full, 1)
                    if s % 4 == 3 and s // 4 + 2 < PAIRS:
                        keys(b, s // 4 + 2)
                    j, r = divmod(s - 13, 4)
                    if 0 <= j < PAIRS - 1 and r == 0:
                        output(b, j)

            def batch(b):
                router = not is_zero(b)
                pe.wait_ge(x_split, b + 1)
                for k in range(KC):
                    project(b, f"lin_q{k}", [((0, S), part(wqkv, slice(k * P, k * P + P)), x_t)])
                if router:
                    output(b - 1, PAIRS - 1)
                for t in range(TT):
                    project(b, f"lin_kv{t}", [((0, 512), part(x_t, slice(t * P, t * P + P)),
                                               part(wqkv, slice(C, 3 * C)))])
                pe.wait_ge(f_split, b + 1)
                values(b, 0)
                values(b, 1)
                ps, full = fill(b, "lin_sum")
                read(b, "lin_kv0")
                read(b, "lin_kv1")
                for k in range(KC):
                    for t in range(TT):
                        mm = pe.matmul(ps[:, k * NL:k * NL + NL], lin_k[:, t, k * P:k * P + P], lin_v[:, t, k, :],
                                       start=(t == 0), stop=(t == TT - 1))
                mm.then_inc(full, 1)
                values(b, 2)
                if is_zero(b):
                    pe.wait_ge(weights_loaded, len(whole) * 16)
                read(b, "lin_sum")
                for t in range(TT):
                    ps, full = fill(b, f"lin_out{t}")
                    for k in range(KC):
                        mm = pe.matmul(ps[:, k * NL:k * NL + NL], lin_q[:, k, t * P:t * P + P], lin_kv[:, k, :],
                                       start=True, stop=True)
                    mm.then_inc(full, 1)
                values(b, 3)
                if router:
                    router_tokens(b - 1)
                pe.wait_ge(lin_a_ready, TT * b + TT)
                transposes(b, lin_a, "lin_t")
                if router:
                    router_logits(b - 1)
                keys(b, 0)
                read(b, "lin_t")
                project(b, "lin_proj", [((t * C, t * C + C), lin_at[:, :, t * P:t * P + P], wproj) for t in range(TT)])
                if router:
                    router_rank(b - 1)
                values(b, 4)
                keys(b, 1)
                pe.wait_ge(x1_ready, b + 1)
                transposes(b, x1, "x1_t")
                values(b, 5)
                read(b, "x1_t")
                queries(b, 0)
                attend(b)

            pe.wait_ge(consts_loaded, 16)
            pe.wait_ge(stage_split, len(stages))
            pe.wait_ge(pool_zeros, 2)
            pe.wait_ge(dve_zeros, 2)
            batch(0)
            with pe.Fori(1, B) as b:
                batch(b)
            output(B - 1, PAIRS - 1)
            router_tokens(B - 1)
            router_logits(B - 1)
            router_rank(B - 1)

        @block.scalar
        def _(act):
            def own(name, b):
                k, n = gen_at(b, name)
                act.wait_ge(gen_full[k], n)
                return gen[k], gen_free[k]

            def flat(t):
                return t[:, :, :].rearrange("p a b -> p (a b)")

            def keys(b, j):
                ps, _ = own(f"k{j}", b)
                for i in range(2):
                    for n, cols in ((1, slice(0, S)), (2, slice(S, NK))):
                        last = act.activation(k_d[half(i), 2 * (j % RING) + i, 0, cols], ps[half(i), cols],
                                              ACT.Identity, bias=col_bias[half(i), n, j:j + 1])
                last.then_inc(rounded, 1)

            def queries(b, j):
                ps, _ = own(f"q{j}", b)
                for i in range(2):
                    rows = slice(i * DK, i * DK + DK)
                    act.activation(q_d[rows, 2 * (j % RING) + i, :], ps[rows, 0:S], ACT.Identity,
                                          bias=col_bias[rows, 0, j:j + 1]).then_inc(rounded, 1)

            def router_tokens(r):
                for k in range(KC):
                    ps, free = own(f"tok_t{k}", r + 1)
                    act.activation(tok_t[:, k, :], ps[:, 0:S], ACT.Copy).then_inc(free, 1)

            def values(b, n):
                t, cols = n // 2, slice(n % 2 * 512, n % 2 * 512 + 512)
                rows = KT_TILES[t]
                ps, free = own(f"v{n}", b)
                act.activation(v_s[0:rows, t, cols], ps[0:rows, :], ACT.Copy).then_inc(free, 1)

            def router_exp(r):
                act.wait_ge(rel_ready, r + 1)
                act.activation(e_rel[:, :, :], rel[:, :, :], ACT.Exp).then_inc(e_rel_ready, 1)

            def batch(b):
                router = not is_zero(b)
                for k in range(KC):
                    ps, free = own(f"lin_q{k}", b)
                    act.activation(e_x[:, k, :], ps[:, 0:C], ACT.Exp).then_inc(exp_ready, 1)
                for t in range(TT):
                    ps, free = own(f"lin_kv{t}", b)
                    act.activation(lin_v[:, t, :, 0:P], ps[:, C:2 * C].rearrange("p (k c) -> p k c", k=KC), ACT.Copy)
                    act.activation(e_x[:, KC + t, :], ps[:, 0:C], ACT.Exp).then_inc(exp_ready, 1)
                values(b, 0)
                values(b, 1)
                values(b, 2)
                values(b, 3)
                if router:
                    router_tokens(b - 1)
                ps, free = own("lin_t", b)
                act.activation(flat(lin_at), ps[:, :], ACT.Copy).then_inc(free, 1)
                if router:
                    router_exp(b - 1)
                if is_zero(b):
                    act.wait_ge(weights_loaded, len(whole) * 16)
                keys(b, 0)
                values(b, 4)
                keys(b, 1)
                ps, _ = own("x1_t", b)
                act.activation(flat(x1_t[0]), ps[:, :], ACT.Copy).then_inc(rounded, 1)
                values(b, 5)
                queries(b, 0)
                for s in range(STEPS + 11):
                    j = s // 4
                    if s < STEPS:
                        wait(act, prt_full, STEPS * b + s - 3)
                        act.wait_ge(masked_ready, STEPS * b + s + 1)
                        act.activation(prob[:, s % 4, 0:NKP], masked[:, s % 2, :], ACT.Exp, bias=low[:, s:s + 1],
                                       scale=-1.0, accum_out=total[:, s:s + 1]).then_inc(prob_ready, 1)
                    if s % 4 == 1 and j + 1 < PAIRS:
                        queries(b, j + 1)
                    n = s - 3
                    if 0 <= n < STEPS:
                        wait(act, out_full, STEPS * b + n - 1)
                        act.wait_ge(prt_full, STEPS * b + n + 1)
                        act.activation(prob_t[:, n % 2, :], prt[n % 2][:, 0:PW], ACT.Copy).then_inc(prob_t_ready, 1)
                    j, r = divmod(s - 11, 4)
                    if 0 <= j < PAIRS and r == 0:
                        ps, _ = own(f"o_t{j}", b)
                        act.activation(o_t[0][:, j % 2, :], ps[:, 0:S], ACT.Copy).then_inc(rounded, 1)
                    if s % 4 == 3 and s // 4 + 2 < PAIRS:
                        keys(b, s // 4 + 2)

            for n, (src, halves) in enumerate(stages):
                act.wait_ge(staged[n % 3], 16 * (n // 3) + 16)
                act.activation(halves[0], v_s[:, n % 3, 0:src.shape[-1]], ACT.Copy).then_inc(stage_rounded, 1)
            act.wait_ge(pool_zeros, 2)
            act.wait_ge(dve_zeros, 2)
            batch(0)
            with act.Fori(1, B) as b:
                batch(b)
            router_tokens(B - 1)
            router_exp(B - 1)

        @block.vector
        def _(dve):
            def own(name, b):
                k, n = gen_at(b, name)
                dve.wait_ge(gen_full[k], n)
                return gen[k], gen_free[k]

            def plain(t):
                return t.bitcast(F32)

            def feature(b, n, name, dst, link):
                ps, free = own(name, b)
                dve.wait_ge(exp_ready, 4 * b + n + 1)
                link(dve.tensor_scalar(e_x[:, n, :], e_x[:, n, :], 1.0, None, ALU.min))
                dve.scalar_tensor_tensor(out=dst, in0=ps[:, 0:C], scalar=0.0, in1=e_x[:, n, :],
                                         op0=ALU.max, op1=ALU.add).then_inc(free, 1)

            def moments(src, st, m, var, link, ready):
                for t in range(TT):
                    last = dve.bn_stats(st[:, t, :], src[:, t, :])
                link(last)
                stand(dve, dve_stood)
                for t in range(TT):
                    last = dve.bn_aggr(m[:, t, :], st[:, t, :])
                link(last)
                dve.tensor_scalar(var[:, :], m[:, :, 1], EPS_LN, None, ALU.add).then_inc(ready, 1)

            def normalise(dst, src, m, rs, ready):
                for t in range(TT):
                    last = dve.tensor_scalar(dst[:, t, :], src[:, t, :], m[:, t, 0:1], rs[:, t:t + 1],
                                             ALU.subtract, ALU.mult)
                last.then_inc(ready, 1)

            def router_choice(r, link):
                ps, free = own("logits", r + 1)
                dve.tensor_copy(logit[:, :, :], ps[:, 0:TT * E].rearrange("p (t e) -> p t e", e=E)).then_inc(free, 1)
                k, n = gen_at(r + 1, "logits")
                dve.wait_ge(gen_free[k], n)
                stand(dve, dve_stood)
                for t in range(TT):
                    last = dve.max(top[:, t, :], logit[:, t, :])
                link(last)
                dve.tensor_tensor(rel[:, :, :], logit[:, :, :], top[:, :, 0:1].to_broadcast([P, TT, E]),
                                  ALU.subtract).then_inc(rel_ready, 1)
                for t in range(TT):
                    last = dve.max_index(top_at[:, t, :], top[:, t, :], logit[:, t, :])
                link(last)
                link(dve.tensor_copy(top_f[:, :], top_at[:, :, 0]))
                link(dve.tensor_tensor(onehot[:, :, :], expert_no.unsqueeze(1).to_broadcast([P, TT, E]),
                                       top_f[:, :].unsqueeze(2).to_broadcast([P, TT, E]), ALU.is_equal))
                dve.tensor_tensor(seen[:, 1, :], seen[:, 0, :], onehot[:, 0, :], ALU.add).then_inc(seen_ready, 1)
                dve.wait_ge(e_rel_ready, r + 1)
                link(dve.tensor_reduce(e_sum[:, :], e_rel[:, :, :], AX.X, ALU.add))
                link(dve.reciprocal(p_top[:, :], e_sum[:, :]))

            def router_ranks(r):
                ps, free = own("rank", r + 1)
                dve.tensor_tensor(own_rank[:, :, :], ps[:, 0:TT * E].rearrange("p (t e) -> p t e", e=E),
                                  onehot[:, :, :], ALU.mult).then_inc(free, 1)

            def router_slots(r, link):
                k, n = gen_at(r + 1, "rank")
                dve.wait_ge(gen_free[k], n)
                link(dve.tensor_reduce(rank[:, :], own_rank[:, :, :], AX.X, ALU.add))
                link(dve.tensor_tensor(seen[:, 0, :], seen[:, 1, :], onehot[:, 1, :], ALU.add))
                link(dve.scalar_tensor_tensor(out=kept_rank[:, :], in0=rank[:, :], scalar=float(CAP), in1=rank[:, :],
                                              op0=ALU.is_lt, op1=ALU.mult))
                link(dve.tensor_scalar(beyond[:, :], rank[:, :], float(CAP), float(2 * E * CAP), ALU.is_ge, ALU.mult))
                link(dve.scalar_tensor_tensor(out=slot_f[:, :], in0=top_f[:, :], scalar=float(CAP), in1=kept_rank[:, :],
                                              op0=ALU.mult, op1=ALU.add))
                dve.wait_ge(scatter_done, r + 1)
                dve.tensor_tensor(scatter_at[:, :], slot_f[:, :], beyond[:, :], ALU.add).then_inc(scatter_ready, 1)
                link(dve.tensor_copy(gather_at[:, bass.ds(r * TT, TT)], slot_f[:, :]))
                link(dve.scalar_tensor_tensor(out=weight[:, bass.ds(r * TT, TT)], in0=rank[:, :], scalar=float(CAP),
                                              in1=p_top[:, :], op0=ALU.is_lt, op1=ALU.mult))

            def keys(b, j):
                ps, free = own(f"k{j}", b)
                dve.wait_ge(rounded, rounded_at(b, f"k{j}"))
                for i in range(2):
                    slot = 2 * (j % RING) + i
                    for n, cols in ((1, slice(0, S)), (2, slice(S, NK))):
                        last = dve.scalar_tensor_tensor(
                            out=k_d[half(i), slot, 1, cols], in0=ps[half(i), cols],
                            scalar=col_bias[half(i), n, j:j + 1], in1=plain(k_d[half(i), slot, 0, cols]),
                            op0=ALU.add, op1=ALU.subtract)
                last.then_inc(free, 1)

            def queries(b, j):
                ps, free = own(f"q{j}", b)
                for i in range(2):
                    dve.wait_ge(rounded, rounded_at(b, f"q{j}" if i else f"q{j}_even"))
                    rows, other = slice(i * DK, i * DK + DK), slice((1 - i) * DK, (1 - i) * DK + DK)
                    slot = 2 * (j % RING) + i
                    last = dve.scalar_tensor_tensor(
                        out=q_d[other, slot, :], in0=ps[rows, 0:S], scalar=col_bias[rows, 0, j:j + 1],
                        in1=plain(q_d[rows, slot, :]), op0=ALU.add, op1=ALU.subtract)
                last.then_inc(free, 1)

            def rest(b, name, hi, lo, cols):
                ps, free = own(name, b)
                dve.wait_ge(rounded, rounded_at(b, name))
                dve.tensor_tensor(lo, ps[:, 0:cols], plain(hi), ALU.subtract).then_inc(free, 1)

            def residual(r, link):
                dve.wait_ge(x1_bias_ready, r + 1)
                dve.wait_ge(o_proj_full, r + 1)
                dve.tensor_tensor(z[:, :, :], o_proj[:, :].rearrange("p (t c) -> p t c", t=TT), x1[:, :, :],
                                  ALU.add).then_inc(o_proj_free, 1)
                dve.wait_ge(o_proj_free, r + 1)
                moments(z, stats, mv, var_eps, link, var_ready)

            def attended(r, link):
                dve.wait_ge(x2_free, r + 1)
                dve.wait_ge(rstd_ready, 2 * r + 2)
                normalise(x2, z, mv, rstd, x2_ready)
                dve.wait_ge(x2_ready, r + 1)
                moments(x2, r_stats, r_mv, r_var, link, r_var_ready)

            def tokens(r):
                dve.wait_ge(scatter_done, r + 1)
                dve.wait_ge(r_rstd_ready, r + 1)
                normalise(tok, x2, r_mv, r_rstd, normed_ready)

            def batch(b):
                router = not is_zero(b)
                link, done = chain(dve, dve_chain, b, CHAIN)
                if router:
                    rlink, rdone = chain(dve, dve_router_chain, b - 1, ROUTER_CHAIN)
                for k in range(KC):
                    feature(b, k, f"lin_q{k}", lin_q[:, k, :], link)
                if router:
                    residual(b - 1, rlink)
                feature(b, KC, "lin_kv0", lin_k[:, 0, :], link)
                feature(b, KC + 1, "lin_kv1", lin_k[:, 1, :], link)
                if router:
                    attended(b - 1, rlink)
                if router:
                    tokens(b - 1)
                ps, free = own("lin_sum", b)
                for k in range(KC):
                    last = dve.tensor_tensor(lin_kv[:, k, :], ps[:, k * NL:k * NL + NL], own_head, ALU.mult)
                last.then_inc(free, 1)
                for t in range(TT):
                    ps, free = own(f"lin_out{t}", b)
                    sums = ps[:, 0:KC * NL].rearrange("p (k c) -> p k c", k=KC)
                    link(dve.tensor_scalar(lin_den[:, t, :, :], sums[:, :, P:NL], EPS_LIN, None, ALU.add))
                    link(dve.reciprocal(lin_den[:, t, :, :], lin_den[:, t, :, :]))
                    for k in range(KC):
                        last = dve.tensor_tensor(
                            lin_a[:, t, k * P:k * P + P].rearrange("p (h d) -> p h d", d=LD),
                            ps[:, k * NL:k * NL + P].rearrange("p (h d) -> p h d", d=LD),
                            lin_den[:, t, k, :].unsqueeze(2).to_broadcast([P, HP, LD]), ALU.mult)
                    last.then_inc(free, 1)
                    k, n = gen_at(b, f"lin_out{t}")
                    dve.wait_ge(gen_free[k], n)
                    dve.sem_inc(lin_a_ready, 1)
                if router:
                    router_choice(b - 1, rlink)
                if is_zero(b):
                    dve.wait_ge(weights_loaded, len(whole) * 16)
                ps, free = own("lin_proj", b)
                dve.wait_ge(x_bias_ready, b + 1)
                dve.tensor_tensor(z[:, :, :], ps[:, :].rearrange("p (t c) -> p t c", t=TT), x_in[:, :, :],
                                  ALU.add).then_inc(free, 1)
                k, n = gen_at(b, "lin_proj")
                dve.wait_ge(gen_free[k], n)
                moments(z, stats, mv, var_eps, link, var_ready)
                if router:
                    router_ranks(b - 1)
                keys(b, 0)
                dve.wait_ge(rstd_ready, 2 * b + 1)
                normalise(x1, z, mv, rstd, x1_ready)
                keys(b, 1)
                rest(b, "x1_t", x1_t[0][:, :, :].rearrange("p a b -> p (a b)"),
                     x1_t[1][:, :, :].rearrange("p a b -> p (a b)"), 512)
                queries(b, 0)
                for s in range(STEPS + 11):
                    j, r = divmod(s - 9, 4)
                    if 0 <= j < PAIRS and r == 0:
                        dve.wait_ge(out_full, STEPS * b + 4 * j + 4)
                        link(dve.reciprocal(inv_total[:, :], total[:, 4 * j:4 * j + 4]))
                        if j >= 2:
                            k, n = gen_at(b, f"o_t{j - 2}")
                            dve.wait_ge(gen_full[k], n)
                        for i in range(2):
                            last = dve.tensor_tensor(
                                o_s[:, j % 2, :, i * DK:i * DK + DK],
                                out_ps[:, i * P:i * P + P].rearrange("p (t d) -> p t d", t=TT),
                                inv_total[:, 2 * i:2 * i + 2].unsqueeze(2).to_broadcast([P, TT, DK]), ALU.mult)
                        last.then_inc(o_ready, 1)
                    j = s // 4
                    if s < STEPS:
                        wait(dve, prob_ready, STEPS * b + s - 1)
                        if s % 4 == 0:
                            dve.wait_ge(mask_ready, PAIRS * b + j + 1)
                        dve.wait_ge(score_full, STEPS * b + s + 1)
                        stand(dve, dve_stood)
                        dve.tensor_tensor_reduce(masked[:, s % 2, :], score[s % 2][:, 0:NKP],
                                                 mask_add[:, s % (4 * RING), :], -SCALE, 3e38, ALU.add, ALU.min,
                                                 low[:, s:s + 1]).then_inc(masked_ready, 1)
                    if s == 3 and router:
                        router_slots(b - 1, rlink)
                        assert rdone[0] == ROUTER_CHAIN, rdone
                    if s % 4 == 1 and 2 <= j + 1 < PAIRS:
                        keys(b, j + 1)
                    if s % 4 == 2 and j + 1 < PAIRS:
                        queries(b, j + 1)
                    j, r = divmod(s - 12, 4)
                    if 0 <= j < PAIRS and r == 0:
                        rest(b, f"o_t{j}", o_t[0][:, j % 2, :], o_t[1][:, j % 2, :], S)
                assert done[0] == CHAIN, done

            dve.memset(k_d[:, :, :, NK:NKP].bitcast(F32), 0.0).then_inc(dve_zeros, 1)
            dve.memset(seen[:, :, :], 0.0).then_inc(dve_zeros, 1)
            for n, (src, halves) in enumerate(stages):
                dve.wait_ge(stage_rounded, n + 1)
                dve.tensor_tensor(halves[1], v_s[:, n % 3, 0:src.shape[-1]], plain(halves[0]),
                                  ALU.subtract).then_inc(stage_split, 1)
            dve.wait_ge(stage_split, len(stages))
            dve.wait_ge(dve_zeros, 2)
            dve.wait_ge(consts_loaded, 16)
            batch(0)
            with dve.Fori(1, B) as b:
                batch(b)
            rlink, _ = chain(dve, dve_router_chain, B - 1, ROUTER_CHAIN)
            residual(B - 1, rlink)
            attended(B - 1, rlink)
            tokens(B - 1)
            router_choice(B - 1, rlink)
            router_ranks(B - 1)
            router_slots(B - 1, rlink)

        @block.gpsimd
        def _(pool):
            def power(dst, src, ready):
                pool.tensor_tensor(dst[:, :], src[:, :], half_pow[:, :], ALU.pow).then_inc(ready, 1)

            def mask(b, j):
                u = j // 2
                if j % 2 == 0:
                    pool.wait_ge(mask_loaded[u % 2], 16 * (2 * b + u // 2 + 1))
                wait(pool, masked_ready, STEPS * b + 4 * (j - RING) + 4)
                stand(pool, pool_stood)
                slot, part = j % RING * 4, j % 2 * 4
                pool.tensor_scalar(mask_add[:, slot:slot + 4, 0:S], mask_in[:, u % 2, part:part + 4, :], MASKED, 1.0,
                                   ALU.mult, ALU.mult).then_inc(mask_ready, 1)

            def values(b, n):
                t, cols = n // 2, slice(n % 2 * 512, n % 2 * 512 + 512)
                rows = KT_TILES[t]
                k, full = gen_at(b, f"v{n}")
                pool.wait_ge(gen_free[k], full)
                pool.tensor_tensor(v_s[0:rows, t, cols], v_s[0:rows, t, cols], v_bias[0:rows, t // 2, cols],
                                   ALU.add).then_inc(values_ready, 1)

            def split_in(b, src, halves, loaded, half, ready):
                pool.wait_ge(loaded, 16 * b + 16)
                stand(pool, pool_stood)
                pool.tensor_copy(halves[0][:, :, :], src).then_inc(half, 1)
                pool.wait_ge(half, b + 1)
                pool.tensor_tensor(halves[1][:, :, :], src, halves[0][:, :, :].bitcast(F32),
                                   ALU.subtract).then_inc(ready, 1)

            def split_x(b):
                if not is_zero(b):
                    k, n = gen_at(b - 1, "lin_kv1")
                    pool.wait_ge(gen_full[k], n)
                split_in(b, x_t_in[:, :, :], x_t, x_t_loaded, x_rounded, x_split)

            def split_f(b):
                split_in(b, f_t_in[:, :, 0:S], f_t, f_t_loaded, f_rounded, f_split)

            def router_root(r):
                pool.wait_ge(r_var_ready, r + 1)
                power(r_rstd, r_var, r_rstd_ready)

            def router_affine(r):
                pool.wait_ge(normed_ready, r + 1)
                for n, op in ((2, ALU.mult), (3, ALU.add)):
                    for t in range(TT):
                        last = pool.tensor_tensor(tok[:, t, :], tok[:, t, :], row_bias[:, n, :], op)
                    if n == 2:
                        last.then_inc(affine_half, 1)
                        pool.wait_ge(affine_half, r + 1)
                last.then_inc(tok_ready, 1)

            def router_scatter(r):
                pool.wait_ge(scatter_ready, r + 1)
                pool.wait_ge(tok_ready, r + 1)
                stand(pool, pool_stood)
                for t in range(TT):
                    pool.indirect_dma_start(
                        out=slots_dram, out_offset=bass.IndirectOffsetOnAxis(ap=scatter_at[:, t:t + 1], axis=0),
                        in_=tok[:, t, :], in_offset=None, bounds_check=last_slot, oob_is_err=False
                    ).then_inc(scattered, 16)

            def batch(b, last_batch=False):
                router = not is_zero(b)
                if router:
                    pool.wait_ge(var_ready, 2 * b)
                    power(rstd, var_eps, rstd_ready)
                    router_root(b - 1)
                    router_affine(b - 1)
                pool.wait_ge(x_loaded, 16 * b + 16)
                for t in range(TT):
                    last = pool.tensor_tensor(x_in[:, t, :], x_in[:, t, :], row_bias[:, 0, :], ALU.add)
                last.then_inc(x_bias_ready, 1)
                values(b, 0)
                values(b, 1)
                mask(b, 0)
                mask(b, 1)
                values(b, 2)
                values(b, 3)
                pool.wait_ge(var_ready, 2 * b + 1)
                power(rstd, var_eps, rstd_ready)
                values(b, 4)
                values(b, 5)
                k, n = gen_at(b, "x1_t")
                pool.wait_ge(gen_full[k], n)
                for t in range(TT):
                    last = pool.tensor_tensor(x1[:, t, :], x1[:, t, :], row_bias[:, 1, :], ALU.add)
                last.then_inc(x1_bias_ready, 1)
                for j in range(2, PAIRS):
                    mask(b, j)
                    if j == 2 and router:
                        router_scatter(b - 1)
                    if j == 4 and not last_batch:
                        split_x(b + 1)
                if not last_batch:
                    split_f(b + 1)
                if router:
                    pool.wait_ge(scattered, 32 * b)
                else:
                    pool.wait_ge(slots_zeroed, 16 * ZEROED)
                pool.sem_inc(scatter_done, 1)

            last_slot = pool.to_reg(E * CAP - 1)
            pool.memset(tok[:, :, :], 0.0).then_inc(pool_zeros, 1)
            pool.memset(half_pow[:, :], -0.5)
            pool.memset(mask_add[:, :, S:NK], 0.0)
            pool.memset(mask_add[:, :, NK:NKP], MASKED)
            pool.memset(prob[:, :, NK:PW], 0.0)
            pool.memset(lin_v[:, :, :, P:NL], 1.0).then_inc(pool_zeros, 1)
            pool.wait_ge(pool_zeros, 2)
            split_x(0)
            split_f(0)
            pool.wait_ge(weights_loaded, len(whole) * 16)
            batch(0)
            with pool.Fori(1, B - 1) as b:
                batch(b)
            batch(B - 1, last_batch=True)
            pool.wait_ge(var_ready, 2 * B)
            power(rstd, var_eps, rstd_ready)
            router_root(B - 1)
            router_affine(B - 1)
            router_scatter(B - 1)
            pool.wait_ge(scattered, 32 * B)


def half(i):
    return slice(i * DK, i * DK + DK)


def is_zero(b):
    return isinstance(b, int) and b == 0


def batch_of(ap, b, rows=slice(None)):
    return ap[bass.ds(b, 1), :, rows, :].rearrange("b p r c -> p (b r) c")


def experts(nc, io, consts, slots_dram, rows_dram):
    with ExitStack() as ctx:
        def sb(name, shape, dt=F32):
            return ctx.enter_context(nc.sbuf_tensor(name, shape, dt))

        def split(name, shape):
            return sb(name + "_hi", shape, F32R), sb(name + "_lo", shape, F32R)

        def sem(name):
            return ctx.enter_context(nc.semaphore(name))

        def flat(t):
            return t[:, :, :].rearrange("p a b -> p (a b)")

        ident = consts[:, 0:P]
        wi_in = [sb(f"wi_in{i}", [P, KC, I]) for i in range(2)]
        wo_in = [sb(f"wo_in{i}", [P, IT, C]) for i in range(2)]
        slots_in = [sb(f"slots_in{i}", [P, ST, C]) for i in range(2)]
        wi = [split(f"wi{i}", [P, KC, I]) for i in range(2)]
        wo = [split(f"wo_e{i}", [P, IT, C]) for i in range(2)]
        slots_t = split("slots_t", [P, KC, CAP])
        gelu = sb("gelu", [P, 2, CAP])
        hidden = split("hidden", [P, IT, CAP])
        rows = sb("rows", [P, ST, C])
        ps_t = [ctx.enter_context(nc.psum_tensor(f"ps_t{i}", [P, 512], F32)) for i in range(2)]
        ps_h = [ctx.enter_context(nc.psum_tensor(f"ps_h{i}", [P, 512], F32)) for i in range(2)]
        ps_o = [ctx.enter_context(nc.psum_tensor(f"ps_o{i}", [P, 512], F32)) for i in range(2)]
        slots_loaded = [sem("slots_loaded0"), sem("slots_loaded1")]
        wi_loaded = [sem("wi_loaded0"), sem("wi_loaded1")]
        wo_loaded = [sem("wo_loaded0"), sem("wo_loaded1")]
        weight_rounded, weight_split = sem("weight_rounded"), sem("weight_split")
        t_full, slots_rounded, slots_split = sem("t_full"), sem("slots_rounded"), sem("slots_split")
        h_full, gelu_ready = sem("h_full"), sem("gelu_ready")
        hidden_rounded, hidden_split = sem("hidden_rounded"), sem("hidden_split")
        o_full, o_ready = sem("o_full_e"), sem("o_ready_e")
        rows_stored, e_stood = sem("rows_stored"), sem("e_stood")
        slot_tiles = slots_dram.rearrange("(e t p) c -> e p t c", t=ST, p=P)
        row_tiles = rows_dram.rearrange("(e t p) c -> e p t c", t=ST, p=P)
        PIECES = IT
        PIECE = 2 * KC * I // PIECES

        def piece(i, n):
            src, halves = (wi_in[i], wi[i]) if n < PIECES // 2 else (wo_in[i], wo[i])
            cols = slice(n % (PIECES // 2) * PIECE, (n % (PIECES // 2) + 1) * PIECE)
            return [flat(t)[:, cols] for t in (src,) + halves]

        block = ctx.enter_context(nc.Block())

        def all_experts(eng, expert):
            for i in range(2):
                expert(0, i, False)
            with eng.Fori(1, E // 2 - 1) as g:
                for i in range(2):
                    expert(g, i, False)
            for i in range(2):
                expert(E // 2 - 1, i, i == 1)

        def following(g, i):
            return (g, 1) if i == 0 else (g + 1, 0)

        @block.sync
        def _(sp):
            def load(g, i):
                e = 2 * g + i
                wait(sp, t_full, KC * (e - 2) + KC)
                wait(sp, weight_split, PIECES * (e - 2) + PIECES)
                stand(sp, e_stood)
                sp.dma_start(slots_in[i][:, :, :], batch_of(slot_tiles, e)).then_inc(slots_loaded[i], 16)
                sp.dma_start(wi_in[i][:, :, :], batch_of(io["wi"], e)).then_inc(wi_loaded[i], 16)
                sp.dma_start(wo_in[i][:, :, :], batch_of(io["wo_e"], e)).then_inc(wo_loaded[i], 16)

            def store(g, i):
                e = 2 * g + i
                sp.wait_ge(o_ready, 2 * e + 2)
                stand(sp, e_stood)
                sp.dma_start(batch_of(row_tiles, e), rows[:, :, :]).then_inc(rows_stored, 16)

            load(0, 0)
            load(0, 1)
            load(1, 0)
            load(1, 1)
            with sp.Fori(2, E // 2) as g:
                for i in range(2):
                    store(g - 2, i)
                    load(g, i)
            for g in (E // 2 - 2, E // 2 - 1):
                for i in range(2):
                    store(g, i)
            sp.wait_ge(rows_stored, 16 * E)

        @block.tensor
        def _(pe):
            def products(out, lhs, rhs, first, last):
                terms = [(lhs[0], rhs[0]), (lhs[0], rhs[1]), (lhs[1], rhs[0])]
                for n, (x, y) in enumerate(terms):
                    mm = pe.matmul(out, x, y, start=first and n == 0, stop=last and n == 2)
                return mm

            def transposes(g, i):
                pe.wait_ge(slots_loaded[i], 16 * g + 16)
                for k in range(KC):
                    for t in range(ST):
                        mm = pe.transpose(ps_t[k][:, t * P:t * P + P], slots_in[i][:, t, k * P:k * P + P], ident)
                    mm.then_inc(t_full, 1)

            def expert(g, i, last):
                e = 2 * g + i
                pe.wait_ge(slots_split, KC * e + KC)
                pe.wait_ge(weight_split, PIECES * e + PIECES // 2)
                for f in range(IT):
                    wait(pe, gelu_ready, IT * e + f - 1)
                    for k in range(KC):
                        mm = products(ps_h[f % 2][:, :], [w[:, k, f * P:f * P + P] for w in wi[i]],
                                      [x[:, k, :] for x in slots_t], k == 0, k == KC - 1)
                    mm.then_inc(h_full, 1)
                if not last:
                    transposes(*following(g, i))
                pe.wait_ge(weight_split, PIECES * e + PIECES)
                for v in range(ST // 2):
                    wait(pe, o_ready, 2 * e + v - 1)
                    for u in (2 * v, 2 * v + 1):
                        for f in range(IT):
                            if u == 0:
                                pe.wait_ge(hidden_split, IT * e + f + 1)
                            mm = products(ps_o[v][:, (u % 2) * C:(u % 2) * C + C],
                                          [h[:, f, u * P:u * P + P] for h in hidden],
                                          [w[:, f, :] for w in wo[i]], f == 0, f == IT - 1)
                    mm.then_inc(o_full, 1)

            transposes(0, 0)
            all_experts(pe, expert)

        @block.scalar
        def _(act):
            def weight(g, i, n):
                if n % (PIECES // 2) == 0:
                    act.wait_ge(wo_loaded[i] if n else wi_loaded[i], 16 * g + 16)
                src, hi, lo = piece(i, n)
                act.activation(hi, src, ACT.Copy).then_inc(weight_rounded, 1)

            def slots(g, i):
                for k in range(KC):
                    act.wait_ge(t_full, KC * (2 * g + i) + k + 1)
                    act.activation(slots_t[0][:, k, :], ps_t[k][:, :], ACT.Copy).then_inc(slots_rounded, 1)

            def expert(g, i, last):
                e = 2 * g + i
                for f in range(IT):
                    wait(act, hidden_split, IT * e + f - 1)
                    act.wait_ge(h_full, IT * e + f + 1)
                    act.activation(gelu[:, f % 2, :], ps_h[f % 2][:, :], ACT.Gelu).then_inc(gelu_ready, 1)
                    act.wait_ge(gelu_ready, IT * e + f + 1)
                    act.activation(hidden[0][:, f, :], gelu[:, f % 2, :], ACT.Copy).then_inc(hidden_rounded, 1)
                if not last:
                    slots(*following(g, i))
                    for n in range(PIECES):
                        weight(*following(g, i), n)

            slots(0, 0)
            for n in range(PIECES):
                weight(0, 0, n)
            all_experts(act, expert)

        @block.vector
        def _(dve):
            def plain(t):
                return t.bitcast(F32)

            def weight(g, i, n):
                dve.wait_ge(weight_rounded, PIECES * (2 * g + i) + n + 1)
                src, hi, lo = piece(i, n)
                dve.tensor_tensor(lo, src, plain(hi), ALU.subtract).then_inc(weight_split, 1)

            def slots(g, i):
                for k in range(KC):
                    dve.wait_ge(slots_rounded, KC * (2 * g + i) + k + 1)
                    dve.tensor_tensor(slots_t[1][:, k, :], ps_t[k][:, :], plain(slots_t[0][:, k, :]),
                                      ALU.subtract).then_inc(slots_split, 1)

            def expert(g, i, last):
                e = 2 * g + i
                for f in range(IT):
                    dve.wait_ge(hidden_rounded, IT * e + f + 1)
                    dve.tensor_tensor(hidden[1][:, f, :], gelu[:, f % 2, :], plain(hidden[0][:, f, :]),
                                      ALU.subtract).then_inc(hidden_split, 1)
                if not last:
                    slots(*following(g, i))
                    for n in range(PIECES):
                        weight(*following(g, i), n)
                for v in range(ST // 2):
                    dve.wait_ge(o_full, 2 * e + v + 1)
                    wait(dve, rows_stored, 16 * e)
                    dve.tensor_copy(rows[:, 2 * v:2 * v + 2, :],
                                    ps_o[v][:, :].rearrange("p (t c) -> p t c", t=2)).then_inc(o_ready, 1)

            slots(0, 0)
            for n in range(PIECES):
                weight(0, 0, n)
            all_experts(dve, expert)


def combine(nc, io, weight, gather_at, half_pow, x2_dram, rows_dram):
    R = 4
    with ExitStack() as ctx:
        def sb(name, shape, dt=F32):
            return ctx.enter_context(nc.sbuf_tensor(name, shape, dt))

        def sem(name):
            return ctx.enter_context(nc.semaphore(name))

        at = sb("at", [P, R, TT], I32)
        w = sb("w", [P, R, TT])
        got = sb("got", [P, R, TT, C])
        base = sb("base", [P, R, TT, C])
        y = sb("y", [P, R, TT, C])
        res = sb("res", [P, R, TT, C])
        st = sb("st", [P, R, TT, 6])
        m = sb("m", [P, R, TT, 2])
        var = sb("var", [P, R, TT])
        root = sb("root", [P, R, TT])
        offset = sb("offset", [P, R, TT])
        at_ready, w_ready = sem("at_ready"), sem("w_ready")
        gathered = [sem(f"gathered{i}") for i in range(R)]
        base_in = [sem(f"base_in{i}") for i in range(R)]
        stored = [sem(f"stored{i}") for i in range(R)]
        y_ready, var_done, root_done = sem("y_ready"), sem("var_done"), sem("root_done")
        offset_ready, res_ready = sem("offset_ready"), sem("res_ready")
        steps, stood, c_sp_stood, c_pool_stood = (
            sem("c_steps"), sem("c_stood"), sem("c_sp_stood"), sem("c_pool_stood"))
        STEPS_C = 2

        block = ctx.enter_context(nc.Block())

        def rings(eng, batch):
            for i in range(R):
                batch(0, i, i)
            with eng.Fori(1, B // R) as g:
                for i in range(R):
                    batch(g, i, g * R + i)

        @block.sync
        def _(sp):
            def load(g, i, b):
                wait(sp, y_ready, b - R + 1)
                stand(sp, c_sp_stood)
                sp.dma_start(base[:, i, :, :], batch_of(x2_dram, b)).then_inc(base_in[i], 16)

            def store(g, i, b):
                sp.wait_ge(res_ready, b + 1)
                stand(sp, c_sp_stood)
                sp.dma_start(batch_of(io["out"], b), res[:, i, :, :]).then_inc(stored[i], 16)

            for i in range(R):
                load(0, i, i)
            with sp.Fori(1, B // R) as g:
                for i in range(R):
                    load(g, i, g * R + i)
                    store(g - 1, i, g * R + i - R)
            for i in range(R):
                store(B // R - 1, i, B - R + i)
            for i in range(R):
                sp.wait_ge(stored[i], 16 * (B // R))

        @block.gpsimd
        def _(pool):
            last_slot = pool.to_reg(E * CAP - 1)

            def gather(g, i, b):
                pool.wait_ge(at_ready, b + 1)
                wait(pool, y_ready, b - R + 1)
                stand(pool, c_pool_stood)
                for t in range(TT):
                    pool.indirect_dma_start(
                        out=got[:, i, t, :], out_offset=None, in_=rows_dram,
                        in_offset=bass.IndirectOffsetOnAxis(ap=at[:, i, t:t + 1], axis=0),
                        bounds_check=last_slot, oob_is_err=False).then_inc(gathered[i], 16)

            def power(i, b):
                pool.wait_ge(var_done, b + 1)
                pool.tensor_tensor(root[:, i, :], var[:, i, :], half_pow[:, :], ALU.pow).then_inc(root_done, 1)

            gather(0, 0, 0)
            gather(0, 1, 1)
            for i in range(2, R):
                gather(0, i, i)
                power(i - 2, i - 2)
            with pool.Fori(1, B // R) as g:
                for i in range(R):
                    gather(g, i, g * R + i)
                    power((i - 2) % R, g * R + i - 2)
            for b in (B - 2, B - 1):
                power(b % R, b)

        @block.scalar
        def _(act):
            def batch(g, i, b):
                act.wait_ge(offset_ready, b + 1)
                wait(act, stored[i], 16 * g)
                for t in range(TT):
                    last = act.activation(res[:, i, t, :], y[:, i, t, :], ACT.Identity, bias=offset[:, i, t:t + 1],
                                          scale=root[:, i, t:t + 1])
                last.then_inc(res_ready, 1)
            rings(act, batch)

        @block.vector
        def _(dve):
            def pick(g, i, b):
                dve.tensor_copy(at[:, i, :], gather_at[:, bass.ds(b * TT, TT)]).then_inc(at_ready, 1)
                dve.tensor_scalar(w[:, i, :], weight[:, bass.ds(b * TT, TT)], 0.5, None, ALU.mult).then_inc(w_ready, 1)

            def front(g, i, b):
                dve.wait_ge(w_ready, b + 1)
                dve.wait_ge(gathered[i], 32 * g + 32)
                dve.wait_ge(base_in[i], 16 * g + 16)
                wait(dve, res_ready, b - R + 1)
                for t in range(TT):
                    last = dve.scalar_tensor_tensor(out=y[:, i, t, :], in0=got[:, i, t, :], scalar=w[:, i, t:t + 1],
                                                    in1=base[:, i, t, :], op0=ALU.mult, op1=ALU.add)
                last.then_inc(y_ready, 1)
                dve.wait_ge(y_ready, b + 1)
                for t in range(TT):
                    last = dve.bn_stats(st[:, i, t, :], y[:, i, t, :])
                last.then_inc(steps, 1)
                dve.wait_ge(steps, STEPS_C * b + 1)
                stand(dve, stood)
                for t in range(TT):
                    last = dve.bn_aggr(m[:, i, t, :], st[:, i, t, :])
                last.then_inc(steps, 1)
                dve.wait_ge(steps, STEPS_C * b + 2)
                dve.tensor_scalar(var[:, i, :], m[:, i, :, 1], EPS_LN / 4, None, ALU.add).then_inc(var_done, 1)

            def back(i, b):
                dve.wait_ge(root_done, b + 1)
                dve.scalar_tensor_tensor(out=offset[:, i, :], in0=m[:, i, :, 0], scalar=-1.0, in1=root[:, i, :],
                                         op0=ALU.mult, op1=ALU.mult).then_inc(offset_ready, 1)

            def ring(g, last=False):
                for i in range(R):
                    b = g * R + i
                    front(g, i, b)
                    if not last:
                        pick(g + 1, i, b + R)
                    if i >= 2 or not is_zero(g):
                        back((i - 2) % R, b - 2)

            for i in range(R):
                pick(0, i, i)
            ring(0)
            with dve.Fori(1, B // R - 1) as g:
                ring(g)
            ring(B // R - 1, last=True)
            for b in (B - 2, B - 1):
                back(b % R, b)


def _layout(a):
    import numpy as np

    f = {k: np.asarray(v) for k, v in a.items()}

    def channels_first(w):
        return w.T.reshape(-1, P, w.shape[0]).transpose(1, 0, 2)

    def batch_channels_first(v):
        return v.transpose(0, 2, 1).reshape(v.shape[0], KC, P, v.shape[1]).transpose(0, 2, 1, 3)

    def on_all_partitions(*rows):
        return np.broadcast_to(np.stack(rows)[None], (P, len(rows), rows[0].shape[0]))

    head = np.arange(P) // LD
    consts = np.concatenate([
        np.eye(P), np.triu(np.ones((P, P)), 1), np.ones((P, P)),
        head[:, None] == head[None], head[:, None] == np.arange(HP)[None],
        np.broadcast_to(np.arange(E)[None], (P, E))], axis=1).astype(np.float32)
    x = f["x"]
    mask = f["mask_Bx16xSxS_bk1"]
    out = {
        "consts": consts,
        "x": x.reshape(B, TT, P, C).transpose(0, 2, 1, 3),
        "x_t": batch_channels_first(x),
        "f_t": np.concatenate([batch_channels_first(f["fside_BxSxS_0"]), batch_channels_first(f["ctx_1024"])], axis=3),
        "mask": mask.reshape(B, XH, TT, P, S).transpose(0, 3, 1, 2, 4).reshape(B, P, STEPS, S),
        "wqkv": channels_first(f["L0_attn_Wqkv"]),
        "wproj": channels_first(f["L0_attn_Wproj"]),
        "wq": channels_first(f["L0_xattn_Wq"]),
        "wk": channels_first(f["L0_xattn_Wk"]),
        "wgk": channels_first(f["L0_xattn_Wgk"]),
        "wv": channels_first(f["L0_xattn_Wv"]),
        "wgv": channels_first(f["L0_xattn_Wgv"]),
        "wo": channels_first(f["L0_xattn_Wo"]),
        "wgate": channels_first(f["L0_ffn_gate_weight"]),
        "col_bias": np.stack([f["L0_xattn_bq"], f["L0_xattn_bk"], f["L0_xattn_bgk"]]).reshape(3, PAIRS, P).transpose(2, 0, 1),
        "row_bias": on_all_partitions(f["L0_attn_bproj"], f["L0_xattn_bo"], f["L0_ffn_ln_gamma"], f["L0_ffn_ln_beta"]),
        "v_bias": on_all_partitions(f["L0_xattn_bv"], f["L0_xattn_bgv"]),
        "wi": f["L0_ffn_wi"].reshape(E, KC, P, I).transpose(0, 2, 1, 3),
        "wo_e": f["L0_ffn_wo"].reshape(E, IT, P, C).transpose(0, 2, 1, 3),
    }
    return {k: np.ascontiguousarray(v) for k, v in out.items()}


def kernel(**inputs):
    import numpy as np
    import concourse.bacc as bacc
    from concourse.bass_utils import run_bass_kernel_spmd

    arrays = _layout(inputs)
    nc = bacc.Bacc("TRN2", target_bir_lowering=False, num_devices=1)
    io = {name: nc.dram_tensor("in_" + name, a.shape, mybir.dt.from_np(a.dtype), kind="ExternalInput").ap()
          for name, a in arrays.items()}
    io["out"] = nc.dram_tensor("out", (B, P, TT, C), F32, kind="ExternalOutput").ap()
    decoder_kernel(nc, io)
    r = run_bass_kernel_spmd(nc, [{"in_" + name: a for name, a in arrays.items()}], core_ids=[0])
    out = r.results[0]["out"]
    return np.ascontiguousarray(out.transpose(0, 2, 1, 3)).reshape(B, S, C)
```
